# Optimizing a Trainium2 kernel written in Bass

```python
import numpy as np
import jax
import jax.numpy as jnp

def _softmax(x, axis=-1):
    return jax.nn.softmax(x, axis=axis)

def _gelu(x):
    return jax.nn.gelu(x, approximate=True)

def _silu(x):
    return jax.nn.silu(x)

def _sigmoid(x):
    return jax.nn.sigmoid(x)

def _layernorm(x, axis=-1, eps=1e-05):
    m = jnp.mean(x, axis=axis, keepdims=True)
    v = jnp.var(x, axis=axis, keepdims=True)
    return (x - m) / jnp.sqrt(v + eps)

def _scatter_add(tgt, idx, src, axis=0):
    return tgt.at[idx].add(src)

def _segment_sum(src, seg, n):
    return jax.ops.segment_sum(src, seg, n)
kernel_name = 'mk_lm_tower_d1_tok_ids256_r4_009238'

def setup_inputs(seed: int=0):
    np.random.seed(seed)
    _w = jnp.asarray

    def _rec_inputs():
        import jax
        import jax.numpy as jnp
        _rk = jax.random.key(seed)
        x = jax.random.randint(jax.random.fold_in(_rk, 1), (8, 512), 0, 31993, jnp.int32)
        return x
    x = _rec_inputs()

    def _L0_tok_setup():
        import jax, jax.numpy as jnp
        import numpy as np
        VOCAB = 8000
        EMBED_DIM = 64
        NUM_RULES = 100
        BATCH, SEQ = (4, 512)
        key = jax.random.key(seed)
        k1, k2, k3, k4 = jax.random.split(key, 4)
        token_ids = jax.random.randint(k1, (BATCH, SEQ), 0, VOCAB)
        base_embeddings = jax.random.normal(k2, (VOCAB, EMBED_DIM), dtype=jnp.float32)
        rule_transform = jax.random.normal(k3, (NUM_RULES, EMBED_DIM, EMBED_DIM), dtype=jnp.float32)
        token_rules = jax.random.randint(k4, (VOCAB,), 0, NUM_RULES)
        return {'token_ids': token_ids, 'base_embeddings': base_embeddings, 'rule_transform': rule_transform, 'token_rules': token_rules}
    _L0_tok_all = _L0_tok_setup()
    _L0_tok_in = {k: v for k, v in _L0_tok_all.items() if k in ('base_embeddings', 'rule_transform', 'token_rules')}
    del _L0_tok_all

    def _L0_attn_setup():
        import jax, jax.numpy as jnp
        import numpy as np
        from math import sqrt
        DIM = 64
        key = jax.random.key(seed)
        k1, k2, k3, k4 = jax.random.split(key, 4)
        B, T, D, H, R = (2, 1024, DIM, 8, 32)

        def xavier(k, shape, fan_in, fan_out):
            a = sqrt(6.0 / (fan_in + fan_out))
            return jax.random.uniform(k, shape, jnp.float32, -a, a)
        x = jax.random.normal(k1, (B, T, D), jnp.float32)
        Q = xavier(k2, (H, R, D), D, R)
        K = xavier(k3, (H, R, D), D, R)
        VO = xavier(k4, (H, D, D), D, D)
        return {'x': x, 'Q': Q, 'K': K, 'VO': VO}
    _L0_attn_all = _L0_attn_setup()
    _L0_attn_in = {k: v for k, v in _L0_attn_all.items() if k in ('Q', 'K', 'VO')}
    del _L0_attn_all

    def _L0_ffn_setup():
        import jax, jax.numpy as jnp
        import numpy as np
        D_MODEL = 64
        EXPERT_DIM = 128
        NUM_EXPERTS = 8
        TOP_K = 2
        SEQ_LEN = 512
        BATCH = 2
        key = jax.random.key(seed)
        ks = jax.random.split(key, 8)
        s = 0.02
        x = jax.random.normal(ks[0], (SEQ_LEN, BATCH, D_MODEL), dtype=jnp.float32)
        Wg = jax.random.normal(ks[1], (D_MODEL, NUM_EXPERTS), dtype=jnp.float32) * s
        bg = jax.random.normal(ks[2], (NUM_EXPERTS,), dtype=jnp.float32) * s
        bias = jnp.zeros((NUM_EXPERTS,), dtype=jnp.float32)
        W1 = jax.random.normal(ks[3], (NUM_EXPERTS, D_MODEL, EXPERT_DIM), dtype=jnp.float32) * s
        b1 = jax.random.normal(ks[4], (NUM_EXPERTS, EXPERT_DIM), dtype=jnp.float32) * s
        W2 = jax.random.normal(ks[5], (NUM_EXPERTS, EXPERT_DIM, D_MODEL), dtype=jnp.float32) * s
        b2 = jax.random.normal(ks[6], (NUM_EXPERTS, D_MODEL), dtype=jnp.float32) * s
        return {'x': x, 'Wg': Wg, 'bg': bg, 'bias': bias, 'W1': W1, 'b1': b1, 'W2': W2, 'b2': b2}
    _L0_ffn_all = _L0_ffn_setup()
    _L0_ffn_in = {k: v for k, v in _L0_ffn_all.items() if k in ('Wg', 'bg', 'bias', 'W1', 'b1', 'W2', 'b2')}
    del _L0_ffn_all
    return {'x': x, 'L0_tok_base_embeddings': _L0_tok_in['base_embeddings'], 'L0_tok_rule_transform': _L0_tok_in['rule_transform'], 'L0_tok_token_rules': _L0_tok_in['token_rules'], 'L0_attn_Q': _L0_attn_in['Q'], 'L0_attn_K': _L0_attn_in['K'], 'L0_attn_VO': _L0_attn_in['VO'], 'L0_ffn_Wg': _L0_ffn_in['Wg'], 'L0_ffn_bg': _L0_ffn_in['bg'], 'L0_ffn_bias': _L0_ffn_in['bias'], 'L0_ffn_W1': _L0_ffn_in['W1'], 'L0_ffn_b1': _L0_ffn_in['b1'], 'L0_ffn_W2': _L0_ffn_in['W2'], 'L0_ffn_b2': _L0_ffn_in['b2']}

def reference(x, L0_tok_base_embeddings, L0_tok_rule_transform, L0_tok_token_rules, L0_attn_Q, L0_attn_K, L0_attn_VO, L0_ffn_Wg, L0_ffn_bg, L0_ffn_bias, L0_ffn_W1, L0_ffn_b1, L0_ffn_W2, L0_ffn_b2):
    import jax
    import jax.numpy as jnp

    def _L0_tok_ref(token_ids, base_embeddings, rule_transform, token_rules):
        import jax, jax.numpy as jnp
        import numpy as np
        VOCAB = 8000
        EMBED_DIM = 64
        NUM_RULES = 100
        BATCH, SEQ = (4, 512)
        base_embeds = base_embeddings[token_ids]
        rule_indices = token_rules[token_ids]
        rule_matrices = rule_transform[rule_indices]
        return jnp.einsum('bsd,bsde->bse', base_embeds, rule_matrices)

    def _L0_attn_ref(x, Q, K, VO):
        import jax, jax.numpy as jnp
        import numpy as np
        from math import sqrt
        DIM = 64
        d = x.shape[-1]
        q = jnp.einsum('btd,hrd->bhtr', x, Q)
        k = jnp.einsum('bud,hrd->bhur', x, K)
        scores = jnp.einsum('bhtr,bhur->bhtu', q, k) / sqrt(d)
        attn = jax.nn.softmax(scores, axis=-1)
        ctx = jnp.einsum('bhtu,bud->bhtd', attn, x)
        out = jnp.einsum('bhtd,hde->bte', ctx, VO)
        return out

    def _L0_ffn_ref(x, Wg, bg, bias, W1, b1, W2, b2):
        import jax, jax.numpy as jnp
        import numpy as np
        D_MODEL = 64
        EXPERT_DIM = 128
        NUM_EXPERTS = 8
        TOP_K = 2
        SEQ_LEN = 512
        BATCH = 2
        x_flat = x.reshape(-1, D_MODEL)
        gate_logits = x_flat @ Wg + bg + bias
        topk_vals, topk_idx = jax.lax.top_k(gate_logits, TOP_K)
        topk_w = jax.nn.softmax(topk_vals, axis=-1)
        combine = (jax.nn.one_hot(topk_idx, NUM_EXPERTS, dtype=x.dtype) * topk_w[..., None]).sum(axis=1)
        h = jax.nn.relu(jnp.einsum('td,edh->teh', x_flat, W1) + b1)
        y = jnp.einsum('teh,ehd->ted', h, W2) + b2
        out = jnp.einsum('ted,te->td', y, combine)
        return out.reshape(x.shape)
    h = _L0_tok_ref(x, L0_tok_base_embeddings, L0_tok_rule_transform, L0_tok_token_rules)
    h = h + _L0_attn_ref(_layernorm(h, axis=-1), L0_attn_Q, L0_attn_K, L0_attn_VO)
    h = h + _L0_ffn_ref(_layernorm(h, axis=-1), L0_ffn_Wg, L0_ffn_bg, L0_ffn_bias, L0_ffn_W1, L0_ffn_b1, L0_ffn_W2, L0_ffn_b2)
    return h

_drawn_inputs = setup_inputs


def setup_inputs(seed=0):
    import zlib

    import numpy as np

    out = dict(_drawn_inputs(seed))
    spreads = {'L0_ffn_bias': (0.0, 0.8)}
    factors = {'L0_ffn_Wg': 8.0,
     'L0_ffn_bg': 35.63,
     'L0_ffn_W1': 8.0,
     'L0_ffn_b1': 8.0,
     'L0_ffn_W2': 8.0,
     'L0_ffn_b2': 28.39}
    for name, (base, spread) in spreads.items():
        noise = np.random.default_rng([zlib.crc32(name.encode()), seed]).standard_normal(out[name].shape)
        drawn = base * np.exp(spread * noise) if base else spread * noise
        out[name] = jnp.asarray(drawn.astype(out[name].dtype))
    for name, factor in factors.items():
        out[name] = (out[name] * factor).astype(out[name].dtype)
    return out
```

```python
from contextlib import ExitStack

import numpy as np
import concourse.bass as bass
from concourse import mybir


def shape_constants():
    p = np.arange(128)
    eye = np.eye(128)
    upper = (p[:, None] < p[None, :]).astype(np.float64)
    ramp = np.broadcast_to(p[None, :], (128, 128))
    cols = np.stack([p, p + 128], axis=1)
    return np.concatenate([eye, upper, ramp, cols], axis=1).astype(np.float32)


def lm_tower_kernel(nc, x, base_emb, rule_tr, tok_rules, Q, K, VO, Wg, bg, gbias, W1, b1, W2, b2, consts, out):
    F32, F32R, BF16, I32 = mybir.dt.float32, mybir.dt.float32r, mybir.dt.bfloat16, mybir.dt.int32
    ALU, ACT, AX = mybir.AluOpType, mybir.ActivationFunctionType, mybir.AxisListType

    B, T = x.shape
    VOCAB, D = base_emb.shape
    NR = rule_tr.shape[0]
    H, R, _ = Q.shape
    NE, _, HID = W1.shape
    J = T // 128
    NC = B * J
    LO = 64
    HI = VOCAB // LO
    GT = 4
    MAXT = (B * T + NR * 127) // 128
    NG = -(-MAXT // GT)
    NPAIR = H // 2
    EPS = 1e-5
    SC = 1.0 / float(D) ** 0.5
    CB = 5
    NCH = -(-NC // CB)

    ctx = ExitStack()
    with ctx:
        def sb(name, shape, dt=F32):
            return ctx.enter_context(nc.sbuf_tensor(name, shape, dt))

        def sem(name):
            return ctx.enter_context(nc.semaphore(name))

        bank = [ctx.enter_context(nc.psum_tensor(f"bank{i}", [128, 512], F32)) for i in range(8)]
        emb_sorted = nc.dram_tensor("emb_sorted", (NG * GT * 128, D), F32, kind="Internal").ap()
        y_sorted = nc.dram_tensor("y_sorted", (NG * GT * 128, D), F32, kind="Internal").ap()
        hi_dram = nc.dram_tensor("hi_dram", (128, NC), BF16, kind="Internal").ap()

        cst = sb("cst", [128, 386])
        ident, upper_f, ramp_f, part_f = cst[:, 0:128], cst[:, 128:256], cst[:, 256:384], cst[:, 384:386]
        upper = sb("upper", [128, 128], BF16)
        ones_bf = sb("ones_bf", [128, 128], BF16)
        c128_bf = sb("c128_bf", [1, 128], BF16)
        qk_nat = sb("qk_nat", [128, 4, 2, D])
        wqk_h = sb("wqk_h", [128, 4, 128], F32R)
        wqk_l = sb("wqk_l", [128, 4, 128], F32R)
        vo_blk = sb("vo_blk", [128, NPAIR, 2, D])
        vo_row0 = sb("vo_row0", [128, NPAIR, D])
        vtmp = sb("vtmp", [128, 2, 8 * D])
        w1_f = vtmp[:].rearrange("p a n -> p (a n)")
        w1_h = sb("w1_h", [128, NE * HID], F32R)
        w1_l = sb("w1_l", [128, NE * HID], F32R)
        w2_f = sb("w2_f", [HID, NE, D])
        b1_f = sb("b1_f", [HID, NE])
        wg_f = sb("wg_f", [128, NE])
        wg_h = sb("wg_h", [128, NE], F32R)
        wg_l = sb("wg_l", [128, NE], F32R)
        bg_f = sb("bg_f", [128, 2, NE])
        b2_f = sb("b2_f", [33, NE * D])
        b2_r = sb("b2_r", [33, NE * D], F32R)
        ones_r = sb("ones_r", [33, 128], F32R)
        ones_f = sb("ones_f", [128, 128])
        hbuf = sb("hbuf", [128, NC, D])
        xn = sb("xn", [128, NC, 2, D])
        xa = sb("xa", [128, NC, D])
        pos = sb("pos", [128, NC], I32)
        xs = sb("xs", [128, 2, 512], F32R)
        qk_h = sb("qk_h", [128, 4, 512], F32R)
        qk_l = sb("qk_l", [128, 4, 512], F32R)
        mx = sb("mx", [128, 2, 4 * J])
        negm = sb("negm", [4 * J, 2, 128], F32R)
        ctxT = sb("ctxT", [128, 2, NPAIR, 512])
        srow = sb("srow", [8, 512])
        rsum = sb("rsum", [128, J, 2, NPAIR])
        acc = sb("acc", [128, 2, 8 * D])
        ln_c = sb("ln_c", [128, J, D])
        ln_q = sb("ln_q", [128, J, D])
        ln_s = sb("ln_s", [128, 8, J])
        gt = sb("gt", [128, 8, J, NE])
        gs = sb("gs", [128, 8, J])
        gi = sb("gi", [128, NE])
        comb = sb("comb", [128, 2, J, NE])

        with ExitStack() as part:
            def tb(name, shape, dt=F32):
                return part.enter_context(nc.sbuf_tensor(name, shape, dt))

            ids = tb("ids", [128, 4, NC], I32)
            idf = tb("idf", [128, 3, NC])
            hi_bf = tb("hi_bf", [128, NC], BF16)
            hi_b = tb("hi_b", [HI, 128 * NC], BF16)
            ohT = tb("ohT", [HI, 128 * NC], BF16)
            tab_i = tb("tab_i", [HI, LO], I32)
            tab_f = tb("tab_f", [HI, 2, LO])
            tab = tb("tab", [HI, LO], BF16)
            oh_lo = tb("oh_lo", [128, NC, LO])
            rule = tb("rule", [128, NC])
            oh = tb("oh", [128, NC, NR], BF16)
            run = tb("run", [128, NC + 1, NR], BF16)
            sel = ctxT[:].rearrange("p a q t -> p (a q t)")[:, 0:NC * NR].rearrange("p (c r) -> p c r", r=NR)
            cnt = tb("cnt", [128, 4, NR])
            cnt_i = tb("cnt_i", [128, 2, NR], I32)
            tbase = tb("tbase", [1, NR], BF16)
            zero_nr = tb("zero_nr", [128, NR])
            trule = tb("trule", [128, 2])
            trow = tb("trow", [1, 256], I32)
            pos_t = tb("pos_t", [128, 5, NC], I32)
            etok = xn[:, :, 0, :]
            zrow = tb("zrow", [128, NG * GT * D // 4])
            r_sb = tb("r_sb", [D, NR * D])
            e_in = tb("e_in", [128, 4, GT * D])
            eT = tb("eT", [D, 2, 512])
            y_out = tb("y_out", [128, 4, GT * D])
        with ExitStack() as part:
            qs = part.enter_context(nc.sbuf_tensor("qs", [97, 2, H, 512], F32R))
            ks = part.enter_context(nc.sbuf_tensor("ks", [97, 2, H, 512], F32R))
            prob = part.enter_context(nc.sbuf_tensor("prob", [128, 2, J, 2, 512], F32))
        hid = ctx.enter_context(nc.sbuf_tensor("hid", [128, 2, NE, 512], F32))

        names = """cst_in ids_in tab_in rules_in qk_in w_in zero_set zeroed ids_ok hi_ok hi_out hi_in ohT_ok
            tab_ok looked oh_ok run_ok cons_ok ranked tb_ok placed pos_ok trule_ok trowed trow_ok e_got
            scattered eT_ps eT_ok y_ps y_ok stored y_loaded xn_ready xa_ready
            wq_ps wq_h wq_ok w1_h b_set w_ok xT_ps x_hi xs_ready proj_ps qk_hi qk_lo stack_in ks_one s_ps
            mx_done mt_ps negm_ready m_in st_ps exp_done pv_done ctx_copied srow_in rt_ps rsum_ready
            vo_ps vo_used h1_ready gate_ps gate_used gd_ready ge_ready comb_ready up_ps relu_done dn_ps dn_used
            h2_ready out_done dve_chain pool_chain act_chain""".split()
        S = {n: sem(n) for n in names}
        e_in_sem = [sem(f"e_in{i}") for i in range(4)]
        y_out_sem = [sem(f"y_out{i}") for i in range(4)]

        RING = 2

        def aux_at(b, k):
            todo = []
            if k == 1 and 0 <= b < B:
                todo.append(("mt", b, 1))
            if k == 3 and 0 <= b - 1 < B:
                todo.append(("rt", b - 1, 0))
            if k in (4, 6, 8, 10) and 0 <= b - 1 < B:
                todo.append(("vo", b - 1, (k - 4) // 2))
            if k == 10 and 0 <= b + 1 < B:
                todo.append(("mt", b + 1, 0))
            if k == 11 and 0 <= b + 2 < B:
                todo.append(("xT", b + 2, 0))
            if k >= 12 and 0 <= b + 2 < B:
                todo.append(("proj", b + 2, k - 12))
            return todo

        order = [a for b in range(-2, B + 1) for k in range(16) for a in aux_at(b, k)]
        slot = {a: n for n, a in enumerate(order)}

        def ring(a):
            return bank[6 + slot[a] % RING]

        def drained(eng, a):
            n = slot[a] - RING
            if n < 0:
                return
            kind, b, i = order[n]
            if kind == "mt":
                eng.wait_ge(S["negm_ready"], 2 * b + i + 1)
            if kind == "rt":
                eng.wait_ge(S["rsum_ready"], b + 1)
            if kind == "vo":
                eng.wait_ge(S["vo_used"], J * b + i + 1)
            if kind == "xT":
                eng.wait_ge(S["xs_ready"], b + 1)
            if kind == "proj":
                eng.wait_ge(S["qk_lo"], 4 * b + i + 1)

        def s_units(b, k):
            if not 0 <= b + 1 < B or k < 2:
                return []
            first = 3 * (k - 2) if k < 6 else 12 + 2 * (k - 6)
            return range(first, first + (3 if k < 6 else 2))

        NST = 3
        block = ctx.enter_context(nc.Block())

        @block.sync
        def _(sp):
            sp.dma_start(ids[:, 0, :].rearrange("p (b j) -> p b j", j=J), x.rearrange("b (p j) -> p b j", j=J)).then_inc(S["ids_in"], 16)
            sp.dma_start(cst[:], consts).then_inc(S["cst_in"], 16)
            sp.dma_start(tab_i[:], tok_rules.rearrange("(h l) -> h l", l=LO)).then_inc(S["tab_in"], 16)
            sp.wait_ge(S["hi_ok"], 1)
            sp.dma_start(hi_dram, hi_bf[:]).then_inc(S["hi_out"], 16)
            sp.wait_ge(S["hi_out"], 16)
            sp.dma_start(hi_b[:], hi_dram.rearrange("p c -> (p c)").partition_broadcast(HI)).then_inc(S["hi_in"], 16)
            sp.dma_start(r_sb[:].rearrange("d (r e) -> d r e", e=D), rule_tr.rearrange("r d e -> d r e")).then_inc(S["rules_in"], 16)
            es = emb_sorted.rearrange("(g p s) d -> g p (s d)", p=128, s=GT)
            ys = y_sorted.rearrange("(g p s) d -> g p (s d)", p=128, s=GT)
            sp.wait_ge(S["w1_h"], 4)
            sp.wait_ge(S["scattered"], 16 * NC)
            for g in range(NG + 2):
                if g < NG:
                    if g >= 4:
                        sp.wait_ge(S["eT_ps"], g - 3)
                    sp.dma_start(e_in[:, g % 4, :], es[g]).then_inc(e_in_sem[g % 4], 16)
                if g >= 2:
                    q = g - 2
                    sp.wait_ge(S["y_ok"], q + 1)
                    sp.dma_start(ys[q], y_out[:, q % 4, :]).then_inc(y_out_sem[q % 4], 16)
            for i in range(2):
                sp.dma_start(ks[96:97, i, :, :].rearrange("o h (t n) -> o (h t) n", n=128).bitcast(F32),
                             ones_r[0:32, :].bitcast(F32)).then_inc(S["ks_one"], 16)
            for b in range(-2, B + 1):
                nb = b + 1
                if 0 <= nb < B:
                    sp.wait_ge(S["qk_lo"], 4 * nb + 4)
                    if nb >= 2:
                        sp.wait_ge(S["exp_done"], 32 * (nb - 1))
                    for dst, o, parts in ((qs, 0, (qk_h, qk_l, qk_h)), (ks, 2, (qk_h, qk_h, qk_l))):
                        for g in range(4):
                            for s, src in enumerate(parts):
                                sp.dma_start(dst[32 * s:32 * s + 32, nb % 2, g:H:4, :].bitcast(F32),
                                             src[32 * g:32 * g + 32, o:o + 2, :].bitcast(F32)).then_inc(S["stack_in"], 16)
                    sp.wait_ge(S["stack_in"], 384 * (nb + 1))
                if 0 <= b - 1 < B:
                    sp.wait_ge(S["ctx_copied"], NPAIR * b)
                    if b >= 2:
                        sp.wait_ge(S["rt_ps"], b - 1)
                    for hh in range(2):
                        sp.dma_start(srow[4 * hh:4 * hh + 4, :], ctxT[64 * hh:64 * hh + 1, (b - 1) % 2, :, :]).then_inc(S["srow_in"], 16)
                    sp.wait_ge(S["srow_in"], 32 * b)
                if 0 <= b < B:
                    sp.wait_ge(S["negm_ready"], 2 * b + 2)
                    sp.dma_start(qs[96:97, b % 2, 4:8, :].rearrange("o h (t n) -> o (h t) n", n=128).bitcast(F32), negm[:, 1, :].bitcast(F32)).then_inc(S["m_in"], 16)
                    sp.wait_ge(S["m_in"], 32 * b + 32)
                if 0 <= nb < B:
                    sp.wait_ge(S["negm_ready"], 2 * nb + 1)
                    sp.dma_start(qs[96:97, nb % 2, 0:4, :].rearrange("o h (t n) -> o (h t) n", n=128).bitcast(F32), negm[:, 0, :].bitcast(F32)).then_inc(S["m_in"], 16)
                    sp.wait_ge(S["m_in"], 32 * nb + 16)
            for b in range(B):
                sp.wait_ge(S["h2_ready"], J * (b + 1))
                sp.dma_start(out[b].rearrange("(p j) d -> p j d", j=J), hbuf[:, b * J:(b + 1) * J, :]).then_inc(S["out_done"], 16)
            sp.wait_ge(S["out_done"], 16 * B)

        @block.gpsimd
        def _(pool):
            nc.gpsimd.memset(zrow[:], 0.0).then_inc(S["zero_set"], 1)
            nc.gpsimd.memset(ones_f[:], 1.0).then_inc(S["b_set"], 1)
            nc.gpsimd.memset(vo_blk[:], 0.0).then_inc(S["b_set"], 1)
            nc.gpsimd.memset(b2_f[:], 0.0).then_inc(S["b_set"], 1)
            nc.gpsimd.memset(xa[:], 1.0).then_inc(S["b_set"], 1)
            pool.wait_ge(S["ids_ok"], 1)
            for c in range(NC):
                nc.gpsimd.indirect_dma_start(etok[:, c, :], None, base_emb,
                                             bass.IndirectOffsetOnAxis(ap=ids[:, 1, c:c + 1], axis=0)).then_inc(S["e_got"], 16)
            pool.wait_ge(S["e_got"], 16 * NC)
            pool.wait_ge(S["zeroed"], 16 * 4)
            pool.wait_ge(S["pos_ok"], 1)
            for c in range(NC):
                nc.gpsimd.indirect_dma_start(emb_sorted, bass.IndirectOffsetOnAxis(ap=pos[:, c:c + 1], axis=0),
                                             etok[:, c, :], None).then_inc(S["scattered"], 16)
            for q in range(4):
                pool.wait_ge(y_out_sem[q], 16 * len(range(q, NG, 4)))
            for b in range(B):
                for c in range(b * J, (b + 1) * J):
                    nc.gpsimd.indirect_dma_start(hbuf[:, c, :], None, y_sorted,
                                                 bass.IndirectOffsetOnAxis(ap=pos[:, c:c + 1], axis=0)).then_inc(S["y_loaded"], 16)
                pool.wait_ge(S["y_loaded"], 16 * J * (b + 1))
            n = 0

            def fold(c, used, ready):
                nonlocal n
                v, a = vtmp[:, used % 2, :], acc[:, used % 2, :]
                src = v
                width = 4 * D
                at = 0
                while width >= D:
                    nc.gpsimd.tensor_tensor(a[:, at:at + width], src[:, 0:width], src[:, width:2 * width], ALU.add).then_inc(S["pool_chain"], 1)
                    n += 1
                    pool.wait_ge(S["pool_chain"], n)
                    src = a[:, at:at + width]
                    at += width
                    width //= 2
                nc.gpsimd.tensor_tensor(hbuf[:, c, :], hbuf[:, c, :], src, ALU.add).then_inc(S[ready], 1)

            for b in range(-2, B + 1):
                if b + 2 < B:
                    pool.wait_ge(S["xn_ready"], b + 3)
                    c = slice((b + 2) * J, (b + 3) * J)
                    nc.gpsimd.tensor_copy(xa[:, c, 1:D], xn[:, c, 0, 1:D]).then_inc(S["xa_ready"], 1)
                if b >= 1:
                    for c in range((b - 1) * J, b * J):
                        pool.wait_ge(S["vo_used"], c + 1)
                        fold(c, c, "h1_ready")
            for c in range(NC):
                pool.wait_ge(S["dn_used"], c + 1)
                fold(c, c, "h2_ready")

        @block.scalar
        def _(act):
            act.wait_ge(S["zero_set"], 1)
            flat = emb_sorted.rearrange("(z p s) d -> z p (s d)", z=4, p=128)
            for i in range(4):
                act.dma_start(flat[i], zrow[:]).then_inc(S["zeroed"], 16)
            for i, src in enumerate((Q, K)):
                for half in range(2):
                    for dup in range(2):
                        act.dma_start(qk_nat[:, 2 * i + half, dup, :],
                                      src[4 * half:4 * half + 4].rearrange("h r d -> (h r) d")).then_inc(S["qk_in"], 16)
            act.wait_ge(S["b_set"], 4)
            for hh in range(2):
                act.dma_start(vo_blk[64 * hh:64 * hh + 64, :, hh, :],
                              VO.rearrange("(q t) d e -> t d q e", t=2)[hh]).then_inc(S["w_in"], 16)
                act.dma_start(vo_row0[64 * hh:64 * hh + 64, :, :],
                              VO.rearrange("(q t) d e -> t d q e", t=2)[hh, 0].partition_broadcast(64)).then_inc(S["w_in"], 16)
                act.dma_start(w1_f[64 * hh:64 * hh + 64, :].rearrange("d (e n) -> d e n", n=HID),
                              W1.rearrange("e d n -> d e n")).then_inc(S["w_in"], 16)
                act.dma_start(wg_f[64 * hh:64 * hh + 64, :], Wg).then_inc(S["w_in"], 16)
                act.dma_start(b2_f[32 * hh:32 * hh + 1, :], b2.rearrange("(o e) d -> o (e d)", o=1)).then_inc(S["w_in"], 16)
            act.dma_start(w2_f[:], W2.rearrange("e n d -> n e d")).then_inc(S["w_in"], 16)
            act.dma_start(bg_f[:, 0, :], bg.partition_broadcast(128)).then_inc(S["w_in"], 16)
            act.dma_start(bg_f[:, 1, :], gbias.partition_broadcast(128)).then_inc(S["w_in"], 16)
            with nc.allow_non_contiguous_dma(reason="one small transposed load"):
                act.dma_start(b1_f[:], b1.rearrange("e n -> n e")).then_inc(S["w_in"], 16)
            act.wait_ge(S["wq_ps"], 1)
            nc.scalar.copy(wqk_h[:].rearrange("p o n -> p (o n)"), bank[7][:]).then_inc(S["wq_h"], 1)
            act.wait_ge(S["w_in"], 16 * 14)
            nc.scalar.copy(w1_h[:], w1_f).then_inc(S["w1_h"], 1)
            nc.scalar.copy(wg_h[:], wg_f[:]).then_inc(S["w1_h"], 1)
            nc.scalar.copy(b2_r[:], b2_f[:]).then_inc(S["w1_h"], 1)
            nc.scalar.copy(ones_r[:], ones_f[0:33, :]).then_inc(S["w1_h"], 1)
            for g in range(NG):
                act.wait_ge(S["eT_ps"], g + 1)
                if g >= 2:
                    act.wait_ge(S["y_ps"], g - 1)
                nc.scalar.copy(eT[:, g % 2, :], bank[g % 2][0:D, :]).then_inc(S["eT_ok"], 1)
            for b in range(-2, B + 1):
                for k in range(16):
                    for a in aux_at(b, k):
                        kind, ab, i = a
                        if kind == "xT":
                            act.wait_ge(S["xT_ps"], ab + 1)
                            if ab >= 2:
                                act.wait_ge(S["proj_ps"], 4 * (ab - 1))
                            nc.scalar.copy(xs[:, ab % 2, :], ring(a)[:]).then_inc(S["x_hi"], 1)
                        if kind == "proj":
                            act.wait_ge(S["proj_ps"], 4 * ab + i + 1)
                            if ab >= 1:
                                act.wait_ge(S["stack_in"], 384 * ab)
                            nc.scalar.copy(qk_h[:, i, :], ring(a)[:]).then_inc(S["qk_hi"], 1)
                        if kind == "mt":
                            act.wait_ge(S["mt_ps"], 2 * ab + i + 1)
                            if ab >= 1:
                                act.wait_ge(S["m_in"], 32 * ab - 16 + 16 * i)
                            nc.scalar.mul(negm[:, i, :], ring(a)[0:4 * J, 0:128], -1.0).then_inc(S["negm_ready"], 1)
                    step = 16 * b + k + 1
                    for u in (2 * step, 2 * step + 1):
                        if 0 <= u < 32 * B:
                            pair, ut, hh = u // 8, u // 2 % 4, u % 2
                            act.wait_ge(S["st_ps"], u + 1)
                            if pair >= 2:
                                act.wait_ge(S["pv_done"], pair - 1)
                            nc.scalar.activation(prob[:, pair % 2, ut, hh, :], bank[u % NST][:], ACT.Exp,
                                                 scale=SC).then_inc(S["exp_done"], 1)
                    if k % 4 == 3 and 0 <= b < B:
                        pair = k // 4
                        act.wait_ge(S["pv_done"], NPAIR * b + pair + 1)
                        if b >= 2:
                            act.wait_ge(S["vo_ps"], J * (b - 1))
                            act.wait_ge(S["srow_in"], 32 * (b - 1))
                        nc.scalar.copy(ctxT[:, b % 2, pair, :], bank[5][:]).then_inc(S["ctx_copied"], 1)
            for b in range(B):
                act.wait_ge(S["xT_ps"], B + b + 1)
                if b >= 2:
                    act.wait_ge(S["up_ps"], NE * (b - 1))
                nc.scalar.copy(xs[:, b % 2, :], bank[6][:]).then_inc(S["x_hi"], 1)
                for e in range(NE):
                    u = NE * b + e
                    act.wait_ge(S["up_ps"], u + 1)
                    if b >= 2:
                        act.wait_ge(S["dn_ps"], J * (b - 1))
                    nc.scalar.activation(hid[:, b % 2, e, :], bank[u % NST][:], ACT.Relu,
                                         bias=b1_f[:, e:e + 1]).then_inc(S["relu_done"], 1)
                    if e == 3:
                        act.wait_ge(S["gd_ready"], b + 1)
                        nc.scalar.activation(gs[:, 5, :], gs[:, 4, :], ACT.Exp).then_inc(S["ge_ready"], 1)

        @block.vector
        def _(dve):
            V = nc.vector
            chain = [0]

            def link(ins):
                chain[0] += 1
                ins.then_inc(S["dve_chain"], 1)
                dve.wait_ge(S["dve_chain"], chain[0])

            def wrap_clamp(f, tmp, size):
                link(V.tensor_scalar(tmp, f, 0.0, float(size), ALU.is_lt, ALU.mult))
                link(V.tensor_tensor(f, f, tmp, ALU.add))
                link(V.tensor_scalar(f, f, 0.0, float(size - 1), ALU.max, ALU.min))

            dve.wait_ge(S["ids_in"], 16)
            f, t = idf[:, 0, :], idf[:, 1, :]
            link(V.tensor_copy(f, ids[:, 0, :]))
            wrap_clamp(f, t, VOCAB)
            V.tensor_copy(ids[:, 1, :], f).then_inc(S["ids_ok"], 1)
            dve.wait_ge(S["ids_ok"], 1)
            link(V.tensor_scalar(ids[:, 2, :], ids[:, 1, :], 6, None, ALU.logical_shift_right))
            V.tensor_copy(hi_bf[:], ids[:, 2, :]).then_inc(S["hi_ok"], 1)
            link(V.tensor_scalar(ids[:, 3, :], ids[:, 1, :], LO - 1, None, ALU.bitwise_and))
            link(V.tensor_copy(idf[:, 2, :], ids[:, 3, :]))
            dve.wait_ge(S["cst_in"], 16)
            link(V.tensor_tensor(oh_lo[:], ramp_f[:, 0:LO].unsqueeze(1).to_broadcast([128, NC, LO]),
                                 idf[:, 2, :].unsqueeze(2).to_broadcast([128, NC, LO]), ALU.is_equal))
            dve.wait_ge(S["tab_in"], 16)
            link(V.tensor_copy(tab_f[:, 0, :], tab_i[:]))
            wrap_clamp(tab_f[:, 0, :], tab_f[:, 1, :], NR)
            V.tensor_copy(tab[:], tab_f[:, 0, :]).then_inc(S["tab_ok"], 1)
            V.tensor_copy(upper[:], upper_f).then_inc(S["cons_ok"], 1)
            V.memset(ones_bf[:], 1.0).then_inc(S["cons_ok"], 1)
            V.memset(c128_bf[:], 128.0).then_inc(S["cons_ok"], 1)
            link(V.memset(run[:, 0, :], 0.0))
            link(V.memset(zero_nr[:], 0.0))
            dve.wait_ge(S["hi_in"], 16)
            V.tensor_scalar(ohT[:], hi_b[:], part_f[0:HI, 0:1], None, ALU.is_equal).then_inc(S["ohT_ok"], 1)
            per = 512 // LO
            for q in range(NC // per):
                dve.wait_ge(S["looked"], q + 1)
                v = oh_lo[:, q * per:(q + 1) * per, :].rearrange("p c l -> p (c l)")
                link(V.tensor_tensor(v, bank[q][:], v, ALU.mult))
            link(V.tensor_reduce(rule[:], oh_lo[:], AX.X, ALU.add))
            link(V.tensor_tensor(oh[:], ramp_f[:, 0:NR].unsqueeze(1).to_broadcast([128, NC, NR]),
                                 rule[:].unsqueeze(2).to_broadcast([128, NC, NR]), ALU.is_equal))
            for c in range(NC - 1):
                link(V.tensor_tensor(run[:, c + 1, :], run[:, c, :], oh[:, c, :], ALU.add))
            V.tensor_tensor(run[:, NC, :], run[:, NC - 1, :], oh[:, NC - 1, :], ALU.add).then_inc(S["run_ok"], 1)
            dve.wait_ge(S["wq_h"], 1)
            V.tensor_tensor(wqk_l[:].rearrange("p o n -> p (o n)"), bank[7][:],
                            wqk_h[:].rearrange("p o n -> p (o n)").bitcast(F32), ALU.subtract).then_inc(S["wq_ok"], 1)
            dve.wait_ge(S["ranked"], 1)
            link(V.tensor_scalar(cnt_i[:, 0, :], bank[7][:, 0:NR], 127.0, None, ALU.add))
            link(V.tensor_scalar(cnt_i[:, 1, :], cnt_i[:, 0, :], 7, None, ALU.logical_shift_right))
            link(V.tensor_copy(cnt[:, 0, :], cnt_i[:, 1, :]))
            link(V.tensor_tensor_scan(cnt[:, 1, :], cnt[:, 0, :], zero_nr[:], 0.0, ALU.add, ALU.add))
            V.tensor_tensor(tbase[:], cnt[0:1, 1, :], cnt[0:1, 0, :], ALU.subtract).then_inc(S["tb_ok"], 1)
            for i in range(2):
                link(V.tensor_scalar(cnt[:, 2 + i, :], cnt[:, 1, :], part_f[:, i:i + 1], None, ALU.is_le))
            link(V.tensor_reduce(trule[:], cnt[:, 2:4, :], AX.X, ALU.add))
            V.tensor_scalar(trule[:], trule[:], float(NR - 1), float(D), ALU.min, ALU.mult).then_inc(S["trule_ok"], 1)
            dve.wait_ge(S["placed"], 1)
            for q in range(NCH):
                w = min(CB, NC - q * CB)
                o = oh[:, q * CB:q * CB + w, :].rearrange("p c r -> p (c r)")
                d = sel[:, q * CB:q * CB + w, :].rearrange("p c r -> p (c r)")
                link(V.tensor_tensor(d, bank[q][:, 0:w * NR], o, ALU.mult))
            link(V.tensor_reduce(idf[:, 0, :], sel, AX.X, ALU.add))
            link(V.tensor_copy(pos_t[:, 0, :], idf[:, 0, :]))
            link(V.tensor_scalar(pos_t[:, 1, :], pos_t[:, 0, :], 9, 9, ALU.logical_shift_right, ALU.logical_shift_left))
            link(V.tensor_scalar(pos_t[:, 2, :], pos_t[:, 0, :], 127, 2, ALU.bitwise_and, ALU.logical_shift_left))
            link(V.tensor_scalar(pos_t[:, 3, :], pos_t[:, 0, :], 7, 3, ALU.logical_shift_right, ALU.bitwise_and))
            link(V.tensor_tensor(pos_t[:, 4, :], pos_t[:, 1, :], pos_t[:, 2, :], ALU.bitwise_or))
            V.tensor_tensor(pos[:], pos_t[:, 4, :], pos_t[:, 3, :], ALU.bitwise_or).then_inc(S["pos_ok"], 1)
            dve.wait_ge(S["trowed"], 1)
            V.tensor_copy(trow[:], bank[7][0:1, 0:256]).then_inc(S["trow_ok"], 1)
            dve.wait_ge(S["w1_h"], 4)
            V.tensor_tensor(w1_l[:], w1_f, w1_h[:].bitcast(F32), ALU.subtract).then_inc(S["w_ok"], 1)
            V.tensor_tensor(wg_l[:], wg_f[:], wg_h[:].bitcast(F32), ALU.subtract).then_inc(S["w_ok"], 1)
            V.tensor_tensor(b2_r[32:33, :], b2_f[32:33, :], b2_r[32:33, :].bitcast(F32), ALU.subtract).then_inc(S["w_ok"], 1)
            for hh in range(2):
                r = slice(64 * hh, 64 * hh + 64)
                V.tensor_tensor(vo_blk[r, :, hh, :], vo_blk[r, :, hh, :], vo_row0[r, :, :], ALU.subtract).then_inc(S["w_ok"], 1)
            V.tensor_scalar(gi[:], ramp_f[:, 0:NE], 1000.0, None, ALU.add).then_inc(S["w_ok"], 1)
            for g in range(NG):
                dve.wait_ge(S["y_ps"], g + 1)
                if g >= 4:
                    dve.wait_ge(y_out_sem[g % 4], 16 * (g // 4))
                V.tensor_copy(y_out[:, g % 4, :], bank[2 + g % 2][:, 0:GT * D]).then_inc(S["y_ok"], 1)
            dve.wait_ge(S["scattered"], 16 * NC)

            def layernorm(b, n):
                h4 = hbuf[:, b * J:(b + 1) * J, :]
                wide = [128, J, D]
                s_ = [ln_s[:, i, :] for i in range(8)]
                link(V.tensor_reduce(s_[0], h4, AX.X, ALU.add))
                link(V.tensor_scalar(s_[1], s_[0], 1.0 / D, None, ALU.mult))
                link(V.tensor_tensor(ln_c[:], h4, s_[1].unsqueeze(2).to_broadcast(wide), ALU.subtract))
                link(V.tensor_tensor(ln_q[:], ln_c[:], ln_c[:], ALU.mult))
                link(V.tensor_reduce(s_[2], ln_q[:], AX.X, ALU.add))
                link(V.tensor_scalar(s_[3], s_[2], 1.0 / D, EPS, ALU.mult, ALU.add))
                link(V.tensor_scalar(s_[4].bitcast(I32), s_[3].bitcast(I32), 1, None, ALU.logical_shift_right))
                link(V.tensor_scalar(s_[5].bitcast(I32), s_[4].bitcast(I32), -1.0, float(0x5F3759DF), ALU.mult, ALU.add))
                for _ in range(4):
                    link(V.scalar_tensor_tensor(s_[6], s_[5], -0.5, s_[5], ALU.mult, ALU.mult))
                    link(V.tensor_tensor(s_[7], s_[6], s_[3], ALU.mult))
                    link(V.scalar_tensor_tensor(s_[5], s_[7], 1.5, s_[5], ALU.add, ALU.mult))
                V.tensor_tensor(xn[:, b * J:(b + 1) * J, :, :], ln_c[:].unsqueeze(2).to_broadcast([128, J, 2, D]),
                                s_[5].unsqueeze(2).unsqueeze(3).to_broadcast([128, J, 2, D]), ALU.mult).then_inc(S["xn_ready"], 1)

            for b in range(-2, B + 1):
                if 0 <= b + 2 < B:
                    dve.wait_ge(S["y_loaded"], 16 * J * (b + 3))
                    layernorm(b + 2, b + 3)
                for k in range(16):
                    for u in s_units(b, k):
                        nb = b + 1
                        n = 32 * nb + u
                        h, tt = u // J, u % J
                        dve.wait_ge(S["s_ps"], n + 1)
                        if nb >= 1 and u % 16 == 0:
                            dve.wait_ge(S["mt_ps"], 2 * nb - 1 + u // 16)
                        V.tensor_reduce(mx[:, u // 16, u % 16:u % 16 + 1], bank[3 + n % 2][:], AX.X, ALU.max).then_inc(S["mx_done"], 1)
                    for a in aux_at(b, k):
                        kind, ab, i = a
                        if kind == "xT":
                            dve.wait_ge(S["x_hi"], ab + 1)
                            lo_rows = xs[64:128, ab % 2, :]
                            V.tensor_tensor(lo_rows, ring(a)[64:128, :], lo_rows.bitcast(F32), ALU.subtract).then_inc(S["xs_ready"], 1)
                        if kind == "proj":
                            dve.wait_ge(S["qk_hi"], 4 * ab + i + 1)
                            V.tensor_tensor(qk_l[:, i, :], ring(a)[:], qk_h[:, i, :].bitcast(F32), ALU.subtract).then_inc(S["qk_lo"], 1)
                        if kind == "rt":
                            dve.wait_ge(S["rt_ps"], ab + 1)
                            if ab >= 1:
                                dve.wait_ge(S["vo_used"], J * ab)
                            V.reciprocal(rsum[:].rearrange("p j t q -> p (j t q)"), ring(a)[:, 0:8 * J]).then_inc(S["rsum_ready"], 1)
                        if kind == "vo":
                            n = J * ab + i
                            dve.wait_ge(S["vo_ps"], n + 1)
                            dve.wait_ge(S["rsum_ready"], ab + 1)
                            if n >= 2:
                                dve.wait_ge(S["h1_ready"], n - 1)
                            V.tensor_tensor(vtmp[:, n % 2, :].rearrange("p (q t e) -> p t q e", t=2, e=D),
                                            ring(a)[:].rearrange("p (q t e) -> p t q e", t=2, e=D),
                                            rsum[:, i, :, :].unsqueeze(3).to_broadcast([128, 2, NPAIR, D]),
                                            ALU.mult).then_inc(S["vo_used"], 1)
            def mix(b):
                for j in range(J):
                    n = J * b + j
                    dve.wait_ge(S["dn_ps"], n + 1)
                    if n >= 2:
                        dve.wait_ge(S["h2_ready"], n - 1)
                    V.tensor_tensor(vtmp[:, n % 2, :].rearrange("p (e d) -> p e d", d=D),
                                    bank[3 + n % 2][:].rearrange("p (e d) -> p e d", d=D),
                                    comb[:, b % 2, j, :].unsqueeze(2).to_broadcast([128, NE, D]), ALU.mult).then_inc(S["dn_used"], 1)

            dve.wait_ge(S["h1_ready"], NC)
            for b in range(B):
                dve.wait_ge(S["h1_ready"], J * (b + 1))
                layernorm(b, B + b + 1)
                dve.wait_ge(S["x_hi"], B + b + 1)
                lo_rows = xs[64:128, b % 2, :]
                V.tensor_tensor(lo_rows, bank[6][64:128, :], lo_rows.bitcast(F32), ALU.subtract).then_inc(S["xs_ready"], 1)
                dve.wait_ge(S["gate_ps"], b + 1)
                l, eq, cand, oh1, l2, oh2, t1, t2 = (gt[:, i, :, :] for i in range(8))
                m1, i1, m2, i2, dd, ee, w1_, w2_ = (gs[:, i, :] for i in range(8))
                w3 = [128, J, NE]
                ramp3 = ramp_f[:, 0:NE].unsqueeze(1).to_broadcast(w3)
                gi3 = gi[:].unsqueeze(1).to_broadcast(w3)

                def over_e(v):
                    return v.unsqueeze(2).to_broadcast(w3)

                V.tensor_tensor(l, bank[7][:, 0:J * NE].rearrange("p (j e) -> p j e", e=NE),
                                bg_f[:, 0, :].unsqueeze(1).to_broadcast(w3), ALU.add).then_inc(S["gate_used"], 1)
                dve.wait_ge(S["gate_used"], b + 1)
                link(V.tensor_tensor(l, l, bg_f[:, 1, :].unsqueeze(1).to_broadcast(w3), ALU.add))

                def pick(l_, m_, i_, oh_):
                    link(V.tensor_reduce(m_, l_, AX.X, ALU.max))
                    link(V.tensor_tensor(eq, l_, over_e(m_), ALU.is_equal))
                    link(V.scalar_tensor_tensor(cand, eq, -1000.0, gi3, ALU.mult, ALU.add))
                    link(V.tensor_reduce(i_, cand, AX.X, ALU.min))
                    link(V.tensor_tensor(oh_, ramp3, over_e(i_), ALU.is_equal))

                pick(l, m1, i1, oh1)
                link(V.scalar_tensor_tensor(l2, oh1, -3.0e38, l, ALU.mult, ALU.add))
                pick(l2, m2, i2, oh2)
                V.tensor_tensor(dd, m2, m1, ALU.subtract).then_inc(S["gd_ready"], 1)
                dve.wait_ge(S["ge_ready"], b + 1)
                link(V.tensor_scalar(w2_, ee, 1.0, None, ALU.add))
                link(V.reciprocal(w1_, w2_))
                link(V.tensor_tensor(w2_, ee, w1_, ALU.mult))
                link(V.tensor_tensor(t1, oh1, over_e(w1_), ALU.mult))
                link(V.tensor_tensor(t2, oh2, over_e(w2_), ALU.mult))
                link(V.tensor_tensor(comb[:, b % 2, :, :], t1, t2, ALU.add))
                if b >= 1:
                    mix(b - 1)
            mix(B - 1)

        @block.tensor
        def _(pe):
            M = nc.tensor.matmul
            pe.wait_ge(S["ohT_ok"], 1)
            pe.wait_ge(S["tab_ok"], 1)
            cols = ohT[:].rearrange("h (p c) -> h c p", c=NC)
            per = 512 // LO
            for c in range(NC):
                last = M(bank[c // per][:, c % per * LO:(c % per + 1) * LO], cols[:, c, :], tab[:], start=True, stop=True)
                if c % per == per - 1:
                    last.then_inc(S["looked"], 1)
            pe.wait_ge(S["qk_in"], 16 * 8)
            pe.wait_ge(S["cst_in"], 16)
            for o in range(4):
                last = nc.tensor.transpose(bank[7][:, o * 128:(o + 1) * 128], qk_nat[:, o, :, :].rearrange("p t d -> p (t d)"), ident)
            last.then_inc(S["wq_ps"], 1)
            pe.wait_ge(S["run_ok"], 1)
            pe.wait_ge(S["cons_ok"], 3)
            for q in range(NCH):
                w = min(CB, NC - q * CB)
                M(bank[q][:, 0:w * NR], upper[:], oh[:, q * CB:q * CB + w, :], start=True, stop=False)
                M(bank[q][:, 0:w * NR], ones_bf[:], run[:, q * CB:q * CB + w, :], start=False, stop=False)
            pe.wait_ge(S["wq_ok"], 1)
            M(bank[7][:, 0:NR], ones_bf[:], run[:, NC, :], start=True, stop=True).then_inc(S["ranked"], 1)
            pe.wait_ge(S["tb_ok"], 1)
            for q in range(NCH):
                w = min(CB, NC - q * CB)
                last = M(bank[q][:, 0:w * NR], c128_bf[:], tbase[:].unsqueeze(1).to_broadcast([1, w, NR]), start=False, stop=True)
            last.then_inc(S["placed"], 1)
            pe.wait_ge(S["trule_ok"], 1)
            for i in range(2):
                last = M(bank[7][0:1, i * 128:(i + 1) * 128], trule[:, i:i + 1], ident, start=True, stop=True)
            last.then_inc(S["trowed"], 1)
            pe.wait_ge(S["trow_ok"], 1)
            pe.wait_ge(S["rules_in"], 16)
            for g in range(NG + 1):
                if g < NG:
                    pe.wait_ge(e_in_sem[g % 4], 16 * (g // 4 + 1))
                    if g >= 2:
                        pe.wait_ge(S["eT_ok"], g - 1)
                    for s in range(GT):
                        last = nc.tensor.transpose(bank[g % 2][0:D, s * 128:(s + 1) * 128], e_in[:, g % 4, s * D:(s + 1) * D], ident)
                    last.then_inc(S["eT_ps"], 1)
                if g >= 1:
                    q = g - 1
                    pe.wait_ge(S["eT_ok"], q + 1)
                    if q >= 2:
                        pe.wait_ge(S["y_ok"], q - 1)
                    for s in range(GT):
                        t_ = q * GT + s
                        at = nc.tensor.value_load(trow[0:1, t_:t_ + 1], min_val=0, max_val=(NR - 1) * D)
                        last = M(bank[2 + q % 2][:, s * D:(s + 1) * D], eT[:, q % 2, s * 128:(s + 1) * 128],
                                 r_sb[:, bass.ds(at, D)], start=True, stop=True)
                    last.then_inc(S["y_ps"], 1)

            pe.wait_ge(S["wq_ok"], 1)
            pe.wait_ge(S["w_ok"], 6)

            def aux(a):
                kind, b, i = a
                out_ = ring(a)
                if kind == "xT":
                    pe.wait_ge(S["xn_ready"], b + 1)
                drained(pe, a)
                if kind == "xT":
                    for j in range(J):
                        last = nc.tensor.transpose(out_[:, j * 128:(j + 1) * 128],
                                                   xn[:, b * J + j, :, :].rearrange("p t d -> p (t d)"), ident)
                    last.then_inc(S["xT_ps"], 1)
                if kind == "proj":
                    pe.wait_ge(S["xs_ready"], b + 1)
                    M(out_[:], wqk_h[:, i, :], xs[:, b % 2, :], start=True, stop=False)
                    M(out_[:], wqk_l[:, i, :], xs[:, b % 2, :], start=False, stop=True).then_inc(S["proj_ps"], 1)
                if kind == "mt":
                    pe.wait_ge(S["mx_done"], 32 * b + 16 * (i + 1))
                    nc.tensor.transpose(out_[0:4 * J, 0:128], mx[:, i, :], ident).then_inc(S["mt_ps"], 1)
                if kind == "rt":
                    pe.wait_ge(S["srow_in"], 32 * (b + 1))
                    for j in range(J):
                        last = nc.tensor.transpose(out_[:, j * 8:(j + 1) * 8], srow[:, j * 128:(j + 1) * 128], ident[0:8, 0:8])
                    last.then_inc(S["rt_ps"], 1)
                if kind == "vo":
                    pe.wait_ge(S["ctx_copied"], NPAIR * (b + 1))
                    for pair in range(NPAIR):
                        last = M(out_[:, pair * 128:(pair + 1) * 128], ctxT[:, b % 2, pair, i * 128:(i + 1) * 128],
                                 vo_blk[:, pair, :, :].rearrange("p t e -> p (t e)"), start=True, stop=True)
                    last.then_inc(S["vo_ps"], 1)

            for b in range(-2, B + 1):
                for k in range(16):
                    step = 16 * b + k + 1
                    for u in (2 * step, 2 * step + 1):
                        if 0 <= u < 32 * B:
                            ub, pair, ut, hh = u // 32, u // 8 % 4, u // 2 % 4, u % 2
                            h = 2 * pair + hh
                            pe.wait_ge(S["m_in"], 32 * ub + 16 * (h // 4 + 1))
                            if u >= NST:
                                pe.wait_ge(S["exp_done"], u - NST + 1)
                            M(bank[u % NST][:], ks[:, ub % 2, h, ut * 128:(ut + 1) * 128], qs[:, ub % 2, h, :],
                              start=True, stop=True).then_inc(S["st_ps"], 1)
                    for u in s_units(b, k):
                        nb = b + 1
                        n = 32 * nb + u
                        h, tt = u // J, u % J
                        pe.wait_ge(S["stack_in"], 384 * (nb + 1))
                        if n >= 2:
                            pe.wait_ge(S["mx_done"], n - 1)
                        M(bank[3 + n % 2][:], qs[0:96, nb % 2, h, tt * 128:(tt + 1) * 128], ks[0:96, nb % 2, h, :],
                          start=True, stop=True).then_inc(S["s_ps"], 1)
                    for a in aux_at(b, k):
                        aux(a)
                    if 0 <= b < B:
                        pair, ut = k // 4, k % 4
                        pe.wait_ge(S["exp_done"], 32 * b + 2 * k + 2)
                        pe.wait_ge(S["xa_ready"], b + 1)
                        if ut == 0 and NPAIR * b + pair >= 1:
                            pe.wait_ge(S["ctx_copied"], NPAIR * b + pair)
                        for hh in range(2):
                            last = M(bank[5][64 * hh:64 * hh + 64, :], xa[:, b * J + ut, :],
                                     prob[:, pair % 2, ut, hh, :], start=(ut == 0), stop=(ut == J - 1))
                        if ut == J - 1:
                            last.then_inc(S["pv_done"], 1)
            def down(b, j):
                n = J * b + j
                pe.wait_ge(S["relu_done"], NE * (b + 1))
                if n >= 2:
                    pe.wait_ge(S["dn_used"], n - 1)
                o = bank[3 + n % 2]
                M(o[:], ones_r[:], b2_r[:], start=True, stop=False)
                for e in range(NE):
                    last = M(o[:, e * D:(e + 1) * D], hid[:, b % 2, e, j * 128:(j + 1) * 128], w2_f[:, e, :],
                             start=False, stop=(e == NE - 1))
                last.then_inc(S["dn_ps"], 1)

            for b in range(B):
                pe.wait_ge(S["xn_ready"], B + b + 1)
                if b:
                    pe.wait_ge(S["xs_ready"], B + b)
                else:
                    pe.wait_ge(S["vo_used"], NC)
                    pe.wait_ge(S["exp_done"], 32 * B)
                    pe.wait_ge(S["mx_done"], 32 * B)
                for j in range(J):
                    last = nc.tensor.transpose(bank[6][:, j * 128:(j + 1) * 128],
                                               xn[:, b * J + j, :, :].rearrange("p t d -> p (t d)"), ident)
                last.then_inc(S["xT_ps"], 1)
                pe.wait_ge(S["xs_ready"], B + b + 1)
                if b:
                    pe.wait_ge(S["gate_used"], b)
                for j in range(J):
                    o = bank[7][:, j * NE:(j + 1) * NE]
                    M(o, xs[:, b % 2, j * 128:(j + 1) * 128], wg_h[:], start=True, stop=False)
                    last = M(o, xs[:, b % 2, j * 128:(j + 1) * 128], wg_l[:], start=False, stop=True)
                last.then_inc(S["gate_ps"], 1)
                for e in range(NE):
                    u = NE * b + e
                    if u >= NST:
                        pe.wait_ge(S["relu_done"], u - NST + 1)
                    M(bank[u % NST][:], w1_h[:, e * HID:(e + 1) * HID], xs[:, b % 2, :], start=True, stop=False)
                    M(bank[u % NST][:], w1_l[:, e * HID:(e + 1) * HID], xs[:, b % 2, :], start=False, stop=True).then_inc(S["up_ps"], 1)
                    if b >= 1 and e % 2 == 1:
                        down(b - 1, e // 2)
            for j in range(J):
                down(B - 1, j)


INPUTS = ['x', 'L0_tok_base_embeddings', 'L0_tok_rule_transform', 'L0_tok_token_rules', 'L0_attn_Q', 'L0_attn_K',
          'L0_attn_VO', 'L0_ffn_Wg', 'L0_ffn_bg', 'L0_ffn_bias', 'L0_ffn_W1', 'L0_ffn_b1', 'L0_ffn_W2', 'L0_ffn_b2']


def kernel(**inputs):
    import concourse.bacc as bacc
    from concourse.bass_utils import run_bass_kernel_spmd

    nc = bacc.Bacc("TRN2", target_bir_lowering=False, num_devices=1)
    arrays = {f"in_{name}": np.ascontiguousarray(inputs[name]) for name in INPUTS}
    arrays["in_consts"] = shape_constants()
    args = [nc.dram_tensor(name, a.shape, mybir.dt.from_np(a.dtype), kind="ExternalInput").ap() for name, a in arrays.items()]
    batch, seq = inputs["x"].shape
    width = inputs["L0_tok_base_embeddings"].shape[1]
    out = nc.dram_tensor("out", (batch, seq, width), mybir.dt.float32, kind="ExternalOutput").ap()
    lm_tower_kernel(nc, *args, out)
    return run_bass_kernel_spmd(nc, [arrays], core_ids=[0]).results[0]["out"]
```

```python
from contextlib import ExitStack

import numpy as np
import concourse.bass as bass
from concourse import mybir


def shape_constants():
    p = np.arange(128)
    eye = np.eye(128)
    upper = (p[:, None] < p[None, :]).astype(np.float64)
    ramp = np.broadcast_to(p[None, :], (128, 128))
    cols = np.stack([p, p + 128], axis=1)
    return np.concatenate([eye, upper, ramp, cols], axis=1).astype(np.float32)


def lm_tower_kernel(nc, x, base_emb, rule_tr, tok_rules, Q, K, VO, Wg, bg, gbias, W1, b1, W2, b2, consts, out):
    F32, F32R, BF16, I32 = mybir.dt.float32, mybir.dt.float32r, mybir.dt.bfloat16, mybir.dt.int32
    ALU, ACT, AX = mybir.AluOpType, mybir.ActivationFunctionType, mybir.AxisListType

    B, T = x.shape
    VOCAB, D = base_emb.shape
    NR = rule_tr.shape[0]
    H, R, _ = Q.shape
    NE, _, HID = W1.shape
    J = T // 128
    NC = B * J
    LO = 64
    HI = VOCAB // LO
    TS = 128
    GT = 4
    MAXT = (B * T + NR * (TS - 1)) // TS
    NG = -(-MAXT // GT)
    NE_IN = 8
    NPAIR = H // 2
    EPS = 1e-5
    SC = 1.0 / float(D) ** 0.5
    CB = 5
    NCH = -(-NC // CB)

    ctx = ExitStack()
    with ctx:
        def sb(name, shape, dt=F32):
            return ctx.enter_context(nc.sbuf_tensor(name, shape, dt))

        def sem(name):
            return ctx.enter_context(nc.semaphore(name))

        bank = [ctx.enter_context(nc.psum_tensor(f"bank{i}", [128, 512], F32)) for i in range(8)]
        emb_sorted = nc.dram_tensor("emb_sorted", (NG * GT * 128, D), F32, kind="Internal").ap()
        y_sorted = nc.dram_tensor("y_sorted", (NG * GT * 128, D), F32, kind="Internal").ap()
        hi_dram = nc.dram_tensor("hi_dram", (128, NC), BF16, kind="Internal").ap()

        NPROB = 4
        cst = sb("cst", [128, 386])
        ident, upper_f, ramp_f, part_f = cst[:, 0:128], cst[:, 128:256], cst[:, 256:384], cst[:, 384:386]
        upper = sb("upper", [128, 128], BF16)
        ones_bf = sb("ones_bf", [128, 128], BF16)
        ctile_bf = sb("ctile_bf", [1, 128], BF16)
        qk_nat = sb("qk_nat", [128, 4, 2, D])
        wqk_h = sb("wqk_h", [128, 4, 128], F32R)
        wqk_l = sb("wqk_l", [128, 4, 128], F32R)
        vo_blk = sb("vo_blk", [128, NPAIR, 2, D])
        vo_row0 = sb("vo_row0", [128, NPAIR, D])
        vtmp = sb("vtmp", [128, 2, 8 * D])
        w1_f = vtmp[:].rearrange("p a n -> p (a n)")
        w1_h = sb("w1_h", [128, NE * HID], F32R)
        w1_l = sb("w1_l", [128, NE * HID], F32R)
        w2_f = sb("w2_f", [HID, NE, D])
        b1_f = sb("b1_f", [HID, NE])
        wg_f = sb("wg_f", [128, NE])
        wg_h = sb("wg_h", [128, NE], F32R)
        wg_l = sb("wg_l", [128, NE], F32R)
        bg_f = sb("bg_f", [128, 2, NE])
        b2_f = sb("b2_f", [33, NE * D])
        b2_r = sb("b2_r", [33, NE * D], F32R)
        ones_r = sb("ones_r", [33, 128], F32R)
        ones_f = sb("ones_f", [128, 128])
        hbuf = sb("hbuf", [128, NC, D])
        xn = sb("xn", [128, NC, 2, D])
        xa = sb("xa", [128, NC, D])
        pos = sb("pos", [128, NC], I32)
        xs = sb("xs", [128, 2, 512], F32R)
        qk_h = sb("qk_h", [128, 4, 512], F32R)
        qk_l = sb("qk_l", [128, 4, 512], F32R)
        mx = sb("mx", [128, 2, 4 * J])
        negm = sb("negm", [4 * J, 2, 128], F32R)
        ctxT = sb("ctxT", [128, 2, NPAIR, 512])
        srow = sb("srow", [8, 512])
        rsum = sb("rsum", [128, J, 2, NPAIR])
        acc = sb("acc", [128, 2, 8 * D])
        ln_c = sb("ln_c", [128, J, D])
        ln_q = sb("ln_q", [128, J, D])
        ln_s = sb("ln_s", [128, 8, J])
        gt = sb("gt", [128, 8, J, NE])
        gs = sb("gs", [128, 8, J])
        gi = sb("gi", [128, NE])
        comb = sb("comb", [128, J, NE])
        hid = sb("hid", [HID, NE, 512])

        with ExitStack() as part:
            def tb(name, shape, dt=F32):
                return part.enter_context(nc.sbuf_tensor(name, shape, dt))

            ids = tb("ids", [128, 4, NC], I32)
            idf = tb("idf", [128, 3, NC])
            hi_bf = tb("hi_bf", [128, NC], BF16)
            hi_b = tb("hi_b", [HI, 128 * NC], BF16)
            ohT = tb("ohT", [HI, 128 * NC], BF16)
            tab_i = tb("tab_i", [HI, LO], I32)
            tab_f = tb("tab_f", [HI, 2, LO])
            tab = tb("tab", [HI, LO], BF16)
            oh_lo = tb("oh_lo", [128, NC, LO])
            rule = tb("rule", [128, NC])
            oh = tb("oh", [128, NC, NR], BF16)
            run = tb("run", [128, NC + 1, NR], BF16)
            sel = ctxT[:].rearrange("p a q t -> p (a q t)")[:, 0:NC * NR].rearrange("p (c r) -> p c r", r=NR)
            cnt = tb("cnt", [128, 4, NR])
            cnt_i = tb("cnt_i", [128, 2, NR], I32)
            tbase = tb("tbase", [1, NR], BF16)
            zero_nr = tb("zero_nr", [128, NR])
            trule = tb("trule", [128, 2])
            trow = tb("trow", [1, 256], I32)
            pos_t = tb("pos_t", [128, 5, NC], I32)
            etok = xn[:, :, 0, :]
            zrow = tb("zrow", [128, NG * GT * D // 4])
            r_sb = tb("r_sb", [D, NR * D])
            flat_hid = hid[:].rearrange("p e n -> p (e n)")
            e_in = flat_hid[:, 0:NE_IN * GT * D].rearrange("p (g n) -> p g n", g=NE_IN)
            y_out = flat_hid[:, NE_IN * GT * D:(NE_IN + 4) * GT * D].rearrange("p (g n) -> p g n", g=4)
            eT = tb("eT", [D, 2, 512])
        with ExitStack() as part:
            qs = part.enter_context(nc.sbuf_tensor("qs", [97, 2, H, 512], F32R))
            ks = part.enter_context(nc.sbuf_tensor("ks", [97, 2, H, 512], F32R))
            prob = part.enter_context(nc.sbuf_tensor("prob", [128, NPROB, 2, 512], F32))
        
        names = """xa_set xn2_ready stack_0 stack_1 stack_2 stack_3 cst_in ids_in tab_in rules_in qk_in w_in zero_set zeroed ids_ok hi_ok hi_out hi_in ohT_ok
            tab_ok looked oh_ok run_ok cons_ok ranked tb_ok placed pos_ok trule_ok trowed trow_ok e_got
            scattered eT_ps eT_ok y_ps y_ok stored y_loaded xn_ready xa_ready
            wq_ps wq_h wq_ok w1_h b_set w_ok xT_ps x_hi xs_ready xT2_ps x2_hi xs2_ready proj_ps qk_hi qk_lo ks_one s_ps
            mx_done mt_ps negm_ready m_in st_ps exp_done pv_done ctx_copied srow_in rt_ps rsum_ready
            vo_ps vo_used h1_ready gate_ps gate_used gd_ready ge_ready comb_ready up_ps relu_done dn_ps dn_used
            h2_ready out_done dve_chain pool_chain act_chain""".split()
        S = {n: sem(n) for n in names}
        e_in_sem = [sem(f"e_in{i}") for i in range(NE_IN)]
        y_out_sem = [sem(f"y_out{i}") for i in range(4)]

        RING = 2

        def aux_at(b, k):
            todo = []
            if k == 1 and 0 <= b < B:
                todo.append(("mt", b, 1))
            if k in (0, 1, 3, 5) and 0 <= b - 3 < B:
                todo.append(("down", b - 3, (0, 1, 3, 5).index(k)))
            if k == 2 and 0 <= b + 2 < B:
                todo.append(("xT", b + 2, 0))
            if 3 <= k <= 6 and 0 <= b + 2 < B:
                todo.append(("proj", b + 2, k - 3))
            if k == 7 and 0 <= b - 1 < B:
                todo.append(("rt", b - 1, 0))
            if k == 7 and 0 <= b - 2 < B:
                todo.append(("xT2", b - 2, 0))
            if k == 8 and 0 <= b - 2 < B:
                todo.append(("gate", b - 2, 0))
            if k == 9 and 0 <= b + 1 < B:
                todo.append(("mt", b + 1, 0))
            if k in (8, 10, 11, 12) and 0 <= b - 1 < B:
                todo.append(("vo", b - 1, (8, 10, 11, 12).index(k)))
            if 0 <= b - 2 < B:
                todo += [("up", b - 2, e) for e in range(NE) if (9, 10, 11, 12, 13, 13, 14, 15)[e] == k]
            return todo

        order = [a for b in range(-2, B + 3) for k in range(16) for a in aux_at(b, k)]
        slot = {a: n for n, a in enumerate(order)}

        def ring(a):
            return bank[6 + slot[a] % RING]

        def drained(eng, a):
            n = slot[a] - RING
            if n < 0:
                return
            kind, b, i = order[n]
            if kind == "mt":
                eng.wait_ge(S["negm_ready"], 2 * b + i + 1)
            if kind == "rt":
                eng.wait_ge(S["rsum_ready"], b + 1)
            if kind == "vo":
                eng.wait_ge(S["vo_used"], J * b + i + 1)
            if kind == "xT":
                eng.wait_ge(S["xs_ready"], b + 1)
            if kind == "proj":
                eng.wait_ge(S["qk_lo"], 4 * b + i + 1)
            if kind == "xT2":
                eng.wait_ge(S["xs2_ready"], b + 1)
            if kind == "gate":
                eng.wait_ge(S["gate_used"], b + 1)
            if kind == "up":
                eng.wait_ge(S["relu_done"], NE * b + i + 1)
            if kind == "down":
                eng.wait_ge(S["dn_used"], J * b + i + 1)

        sums = [a for a in order if a[0] in ("vo", "down")]
        term = {a: n for n, a in enumerate(sums)}

        def folded(eng, a):
            if term[a] >= 2:
                kind, b, i = sums[term[a] - 2]
                eng.wait_ge(S["h1_ready" if kind == "vo" else "h2_ready"], J * b + i + 1)

        def s_units(b, k):
            if not 0 <= b + 1 < B:
                return []
            return range(2 * k, 2 * k + 2)

        NST = 3
        block = ctx.enter_context(nc.Block())

        @block.sync
        def _(sp):
            sp.dma_start(ids[:, 0, :].rearrange("p (b j) -> p b j", j=J), x.rearrange("b (p j) -> p b j", j=J)).then_inc(S["ids_in"], 16)
            sp.dma_start(tab_i[:], tok_rules.rearrange("(h l) -> h l", l=LO)).then_inc(S["tab_in"], 16)
            sp.dma_start(cst[:], consts).then_inc(S["cst_in"], 16)
            sp.wait_ge(S["hi_ok"], 1)
            sp.dma_start(hi_dram, hi_bf[:]).then_inc(S["hi_out"], 16)
            sp.wait_ge(S["hi_out"], 16)
            sp.dma_start(hi_b[:], hi_dram.rearrange("p c -> (p c)").partition_broadcast(HI)).then_inc(S["hi_in"], 16)
            sp.dma_start(r_sb[:].rearrange("d (r e) -> d r e", e=D), rule_tr.rearrange("r d e -> d r e")).then_inc(S["rules_in"], 16)
            es = emb_sorted.rearrange("(g p s) d -> g p (s d)", p=128, s=GT)
            ys = y_sorted.rearrange("(g p s) d -> g p (s d)", p=128, s=GT)
            sp.wait_ge(S["w1_h"], 4)
            sp.wait_ge(S["scattered"], 16 * NC)
            for g in range(NG + NE_IN - 2):
                if g < NG:
                    if g >= NE_IN:
                        sp.wait_ge(S["eT_ps"], g - NE_IN + 1)
                    sp.dma_start(e_in[:, g % NE_IN, :], es[g]).then_inc(e_in_sem[g % NE_IN], 16)
                if g >= NE_IN - 2:
                    q = g - NE_IN + 2
                    sp.wait_ge(S["y_ok"], q + 1)
                    sp.dma_start(ys[q], y_out[:, q % 4, :]).then_inc(y_out_sem[q % 4], 16)
            for i in range(2):
                sp.dma_start(ks[96:97, i, :, :].rearrange("o h (t n) -> o (h t) n", n=128).bitcast(F32),
                             ones_r[0:32, :].bitcast(F32)).then_inc(S["ks_one"], 16)
            def stack(b, g):
                if g == 0:
                    sp.wait_ge(S["qk_lo"], 4 * b + 4)
                if b >= 2:
                    sp.wait_ge(S["exp_done"], 32 * (b - 2) + 8 * (g + 1))
                for dst, o, parts in ((qs, 0, (qk_h, qk_l, qk_h)), (ks, 2, (qk_h, qk_h, qk_l))):
                    for s, src in enumerate(parts):
                        sp.dma_start(dst[32 * s:32 * s + 32, b % 2, 2 * g:2 * g + 2, :].bitcast(F32),
                                     src[32 * g:32 * g + 32, o:o + 2, :].bitcast(F32)).then_inc(S[f"stack_{g}"], 16)

            def max_row(b, half):
                sp.wait_ge(S["negm_ready"], 2 * b + half + 1)
                sp.dma_start(qs[96:97, b % 2, 4 * half:4 * half + 4, :].rearrange("o h (t n) -> o (h t) n", n=128).bitcast(F32),
                             negm[:, half, :].bitcast(F32)).then_inc(S["m_in"], 16)
                sp.wait_ge(S["m_in"], 32 * b + 16 * half + 16)

            for b in range(-2, B + 3):
                if 0 <= b - 1 < B:
                    sp.wait_ge(S["ctx_copied"], NPAIR * b)
                    if b >= 2:
                        sp.wait_ge(S["rt_ps"], b - 1)
                    for hh in range(2):
                        sp.dma_start(srow[4 * hh:4 * hh + 4, :], ctxT[64 * hh:64 * hh + 1, (b - 1) % 2, :, :]).then_inc(S["srow_in"], 16)
                    sp.wait_ge(S["srow_in"], 32 * b)
                if 0 <= b < B:
                    max_row(b, 1)
                if 0 <= b + 1 < B:
                    stack(b + 1, 3)
                if 0 <= b + 2 < B:
                    stack(b + 2, 0)
                    stack(b + 2, 1)
                if 0 <= b + 1 < B:
                    max_row(b + 1, 0)
                if 0 <= b + 2 < B:
                    stack(b + 2, 2)
                if 0 <= b - 3 < B:
                    sp.wait_ge(S["h2_ready"], J * (b - 2))
                    sp.dma_start(out[b - 3].rearrange("(p j) d -> p j d", j=J), hbuf[:, (b - 3) * J:(b - 2) * J, :]).then_inc(S["out_done"], 16)
            sp.wait_ge(S["out_done"], 16 * B)

        @block.gpsimd
        def _(pool):
            pool.wait_ge(S["ids_ok"], 1)
            for c in range(NC):
                nc.gpsimd.indirect_dma_start(etok[:, c, :], None, base_emb,
                                             bass.IndirectOffsetOnAxis(ap=ids[:, 1, c:c + 1], axis=0)).then_inc(S["e_got"], 16)
            nc.gpsimd.memset(xa[:], 1.0).then_inc(S["xa_set"], 1)
            pool.wait_ge(S["xa_set"], 1)
            pool.wait_ge(S["e_got"], 16 * NC)
            pool.wait_ge(S["zeroed"], 16 * 4)
            pool.wait_ge(S["pos_ok"], 1)
            for c in range(NC):
                nc.gpsimd.indirect_dma_start(emb_sorted, bass.IndirectOffsetOnAxis(ap=pos[:, c:c + 1], axis=0),
                                             etok[:, c, :], None).then_inc(S["scattered"], 16)
            for q in range(4):
                pool.wait_ge(y_out_sem[q], 16 * len(range(q, NG, 4)))
            for b in range(B):
                for c in range(b * J, (b + 1) * J):
                    nc.gpsimd.indirect_dma_start(hbuf[:, c, :], None, y_sorted,
                                                 bass.IndirectOffsetOnAxis(ap=pos[:, c:c + 1], axis=0)).then_inc(S["y_loaded"], 16)
                pool.wait_ge(S["y_loaded"], 16 * J * (b + 1))
            n = 0

            def fold(a_, done, ready):
                nonlocal n
                _, b, i = a_
                c = J * b + i
                pool.wait_ge(S[done], c + 1)
                v, a = vtmp[:, term[a_] % 2, :], acc[:, term[a_] % 2, :]
                src = v
                width = 4 * D
                at = 0
                while width >= D:
                    nc.gpsimd.tensor_tensor(a[:, at:at + width], src[:, 0:width], src[:, width:2 * width], ALU.add).then_inc(S["pool_chain"], 1)
                    n += 1
                    pool.wait_ge(S["pool_chain"], n)
                    src = a[:, at:at + width]
                    at += width
                    width //= 2
                nc.gpsimd.tensor_tensor(hbuf[:, c, :], hbuf[:, c, :], src, ALU.add).then_inc(S[ready], 1)

            for b in range(-2, B + 3):
                if b + 2 < B:
                    pool.wait_ge(S["xn_ready"], b + 3)
                    c = slice((b + 2) * J, (b + 3) * J)
                    nc.gpsimd.tensor_copy(xa[:, c, 1:D], xn[:, c, 0, 1:D]).then_inc(S["xa_ready"], 1)
                for k in range(16):
                    for a in aux_at(b, k):
                        if a[0] == "vo":
                            fold(a, "vo_used", "h1_ready")
                        if a[0] == "down":
                            fold(a, "dn_used", "h2_ready")

        @block.scalar
        def _(act):
            act.wait_ge(S["hi_in"], 16)
            act.wait_ge(S["zero_set"], 1)
            flat = emb_sorted.rearrange("(z p s) d -> z p (s d)", z=4, p=128)
            for i in range(4):
                act.dma_start(flat[i], zrow[:]).then_inc(S["zeroed"], 16)
            for i, src in enumerate((Q, K)):
                for half in range(2):
                    for dup in range(2):
                        act.dma_start(qk_nat[:, 2 * i + half, dup, :],
                                      src[4 * half:4 * half + 4].rearrange("h r d -> (h r) d")).then_inc(S["qk_in"], 16)
            act.wait_ge(S["b_set"], 3)
            for hh in range(2):
                act.dma_start(vo_blk[64 * hh:64 * hh + 64, :, hh, :],
                              VO.rearrange("(t q) d e -> t d q e", t=2)[hh]).then_inc(S["w_in"], 16)
                act.dma_start(vo_row0[64 * hh:64 * hh + 64, :, :],
                              VO.rearrange("(t q) d e -> t d q e", t=2)[hh, 0].partition_broadcast(64)).then_inc(S["w_in"], 16)
                act.dma_start(w1_f[64 * hh:64 * hh + 64, :].rearrange("d (e n) -> d e n", n=HID),
                              W1.rearrange("e d n -> d e n")).then_inc(S["w_in"], 16)
                act.dma_start(wg_f[64 * hh:64 * hh + 64, :], Wg).then_inc(S["w_in"], 16)
                act.dma_start(b2_f[32 * hh:32 * hh + 1, :], b2.rearrange("(o e) d -> o (e d)", o=1)).then_inc(S["w_in"], 16)
            act.dma_start(w2_f[:], W2.rearrange("e n d -> n e d")).then_inc(S["w_in"], 16)
            act.dma_start(bg_f[:, 0, :], bg.partition_broadcast(128)).then_inc(S["w_in"], 16)
            act.dma_start(bg_f[:, 1, :], gbias.partition_broadcast(128)).then_inc(S["w_in"], 16)
            with nc.allow_non_contiguous_dma(reason="one small transposed load"):
                act.dma_start(b1_f[:], b1.rearrange("e n -> n e")).then_inc(S["w_in"], 16)
            act.wait_ge(S["wq_ps"], 1)
            nc.scalar.copy(wqk_h[:].rearrange("p o n -> p (o n)"), bank[7][:]).then_inc(S["wq_h"], 1)
            act.wait_ge(S["w_in"], 16 * 14)
            nc.scalar.copy(w1_h[:], w1_f).then_inc(S["w1_h"], 1)
            nc.scalar.copy(wg_h[:], wg_f[:]).then_inc(S["w1_h"], 1)
            nc.scalar.copy(b2_r[:], b2_f[:]).then_inc(S["w1_h"], 1)
            nc.scalar.copy(ones_r[:], ones_f[0:33, :]).then_inc(S["w1_h"], 1)
            for g in range(NG):
                act.wait_ge(S["eT_ps"], g + 1)
                if g >= 2:
                    act.wait_ge(S["y_ps"], g - 1)
                for r in range(2):
                    ins = nc.scalar.copy(eT[:, g % 2, r * 256:(r + 1) * 256], bank[g % 2][64 * r:64 * r + 64, 0:256])
                ins.then_inc(S["eT_ok"], 1)
            for b in range(-2, B + 3):
                for k in range(16):
                    step = 16 * b + k + 1
                    for u in (2 * step, 2 * step + 1):
                        if 0 <= u < 32 * B:
                            act.wait_ge(S["st_ps"], u + 1)
                            if step >= NPROB:
                                act.wait_ge(S["pv_done"], step - NPROB + 1)
                            nc.scalar.activation(prob[:, step % NPROB, u % 2, :], bank[u % NST][:], ACT.Exp,
                                                 scale=SC).then_inc(S["exp_done"], 1)
                    if k % 4 == 3 and 0 <= b < B:
                        pair = k // 4
                        act.wait_ge(S["pv_done"], 16 * b + k + 1)
                        if b >= 2:
                            act.wait_ge(S["vo_ps"], J * (b - 1))
                            act.wait_ge(S["srow_in"], 32 * (b - 1))
                        nc.scalar.copy(ctxT[:, b % 2, pair, :], bank[5][:]).then_inc(S["ctx_copied"], 1)
                    for a in aux_at(b, k):
                        kind, ab, i = a
                        if kind == "xT":
                            act.wait_ge(S["xT_ps"], ab + 1)
                            if ab >= 1:
                                act.wait_ge(S["proj_ps"], 4 * ab)
                            nc.scalar.copy(xs[:, 0, :], ring(a)[:]).then_inc(S["x_hi"], 1)
                        if kind == "xT2":
                            act.wait_ge(S["xT2_ps"], ab + 1)
                            if ab >= 1:
                                act.wait_ge(S["up_ps"], NE * ab)
                            nc.scalar.copy(xs[:, 1, :], ring(a)[:]).then_inc(S["x2_hi"], 1)
                        if kind == "up":
                            u = NE * ab + i
                            act.wait_ge(S["up_ps"], u + 1)
                            if ab >= 1:
                                act.wait_ge(S["dn_ps"], J * ab)
                            nc.scalar.activation(hid[:, i, :], ring(a)[:], ACT.Relu, bias=b1_f[:, i:i + 1]).then_inc(S["relu_done"], 1)
                        if kind == "proj":
                            act.wait_ge(S["proj_ps"], 4 * ab + i + 1)
                            if ab >= 1:
                                for g in range(4):
                                    act.wait_ge(S[f"stack_{g}"], 96 * ab)
                            nc.scalar.copy(qk_h[:, i, :], ring(a)[:]).then_inc(S["qk_hi"], 1)
                        if kind == "mt":
                            act.wait_ge(S["mt_ps"], 2 * ab + i + 1)
                            if ab >= 1:
                                act.wait_ge(S["m_in"], 32 * ab - 16 + 16 * i)
                            nc.scalar.mul(negm[:, i, :], ring(a)[0:4 * J, 0:128], -1.0).then_inc(S["negm_ready"], 1)
                    if k == 15 and 0 <= b - 2 < B:
                        act.wait_ge(S["gd_ready"], b - 1)
                        nc.scalar.activation(gs[:, 5, :], gs[:, 4, :], ACT.Exp).then_inc(S["ge_ready"], 1)

        @block.vector
        def _(dve):
            V = nc.vector
            chain = [0]

            def link(ins):
                chain[0] += 1
                ins.then_inc(S["dve_chain"], 1)
                dve.wait_ge(S["dve_chain"], chain[0])

            def wrap_clamp(f, tmp, size):
                link(V.tensor_scalar(tmp, f, 0.0, float(size), ALU.is_lt, ALU.mult))
                link(V.tensor_tensor(f, f, tmp, ALU.add))
                link(V.tensor_scalar(f, f, 0.0, float(size - 1), ALU.max, ALU.min))

            dve.wait_ge(S["ids_in"], 16)
            f, t = idf[:, 0, :], idf[:, 1, :]
            link(V.tensor_copy(f, ids[:, 0, :]))
            wrap_clamp(f, t, VOCAB)
            V.tensor_copy(ids[:, 1, :], f).then_inc(S["ids_ok"], 1)
            dve.wait_ge(S["ids_ok"], 1)
            link(V.tensor_scalar(ids[:, 2, :], ids[:, 1, :], 6, None, ALU.logical_shift_right))
            V.tensor_copy(hi_bf[:], ids[:, 2, :]).then_inc(S["hi_ok"], 1)
            link(V.tensor_scalar(ids[:, 3, :], ids[:, 1, :], LO - 1, None, ALU.bitwise_and))
            link(V.tensor_copy(idf[:, 2, :], ids[:, 3, :]))
            dve.wait_ge(S["cst_in"], 16)
            link(V.tensor_tensor(oh_lo[:], ramp_f[:, 0:LO].unsqueeze(1).to_broadcast([128, NC, LO]),
                                 idf[:, 2, :].unsqueeze(2).to_broadcast([128, NC, LO]), ALU.is_equal))
            V.memset(zrow[:], 0.0).then_inc(S["zero_set"], 1)
            V.memset(ones_f[:], 1.0).then_inc(S["b_set"], 1)
            V.memset(vo_blk[:], 0.0).then_inc(S["b_set"], 1)
            V.memset(b2_f[:], 0.0).then_inc(S["b_set"], 1)
            dve.wait_ge(S["tab_in"], 16)
            link(V.tensor_copy(tab_f[:, 0, :], tab_i[:]))
            wrap_clamp(tab_f[:, 0, :], tab_f[:, 1, :], NR)
            V.tensor_copy(tab[:], tab_f[:, 0, :]).then_inc(S["tab_ok"], 1)
            V.tensor_copy(upper[:], upper_f).then_inc(S["cons_ok"], 1)
            V.memset(ones_bf[:], 1.0).then_inc(S["cons_ok"], 1)
            V.memset(ctile_bf[:], float(TS)).then_inc(S["cons_ok"], 1)
            link(V.memset(run[:, 0, :], 0.0))
            link(V.memset(zero_nr[:], 0.0))
            dve.wait_ge(S["hi_in"], 16)
            V.tensor_scalar(ohT[:], hi_b[:], part_f[0:HI, 0:1], None, ALU.is_equal).then_inc(S["ohT_ok"], 1)
            per = 512 // LO
            for q in range(NC // per):
                dve.wait_ge(S["looked"], q + 1)
                v = oh_lo[:, q * per:(q + 1) * per, :].rearrange("p c l -> p (c l)")
                link(V.tensor_tensor(v, bank[q][:], v, ALU.mult))
            link(V.tensor_reduce(rule[:], oh_lo[:], AX.X, ALU.add))
            link(V.tensor_tensor(oh[:], ramp_f[:, 0:NR].unsqueeze(1).to_broadcast([128, NC, NR]),
                                 rule[:].unsqueeze(2).to_broadcast([128, NC, NR]), ALU.is_equal))
            for c in range(NC - 1):
                link(V.tensor_tensor(run[:, c + 1, :], run[:, c, :], oh[:, c, :], ALU.add))
            V.tensor_tensor(run[:, NC, :], run[:, NC - 1, :], oh[:, NC - 1, :], ALU.add).then_inc(S["run_ok"], 1)
            dve.wait_ge(S["wq_h"], 1)
            V.tensor_tensor(wqk_l[:].rearrange("p o n -> p (o n)"), bank[7][:],
                            wqk_h[:].rearrange("p o n -> p (o n)").bitcast(F32), ALU.subtract).then_inc(S["wq_ok"], 1)
            dve.wait_ge(S["ranked"], 1)
            link(V.tensor_scalar(cnt_i[:, 0, :], bank[7][:, 0:NR], float(TS - 1), None, ALU.add))
            link(V.tensor_scalar(cnt_i[:, 1, :], cnt_i[:, 0, :], 7, None, ALU.logical_shift_right))
            link(V.tensor_copy(cnt[:, 0, :], cnt_i[:, 1, :]))
            link(V.tensor_tensor_scan(cnt[:, 1, :], cnt[:, 0, :], zero_nr[:], 0.0, ALU.add, ALU.add))
            V.tensor_tensor(tbase[:], cnt[0:1, 1, :], cnt[0:1, 0, :], ALU.subtract).then_inc(S["tb_ok"], 1)
            for i in range(2):
                link(V.tensor_scalar(cnt[:, 2 + i, :], cnt[:, 1, :], part_f[:, i:i + 1], None, ALU.is_le))
            link(V.tensor_reduce(trule[:], cnt[:, 2:4, :], AX.X, ALU.add))
            V.tensor_scalar(trule[:], trule[:], float(NR - 1), float(D), ALU.min, ALU.mult).then_inc(S["trule_ok"], 1)
            dve.wait_ge(S["placed"], 1)
            for q in range(NCH):
                w = min(CB, NC - q * CB)
                o = oh[:, q * CB:q * CB + w, :].rearrange("p c r -> p (c r)")
                d = sel[:, q * CB:q * CB + w, :].rearrange("p c r -> p (c r)")
                link(V.tensor_tensor(d, bank[q][:, 0:w * NR], o, ALU.mult))
            link(V.tensor_reduce(idf[:, 0, :], sel, AX.X, ALU.add))
            link(V.tensor_copy(pos_t[:, 0, :], idf[:, 0, :]))
            link(V.tensor_scalar(pos_t[:, 1, :], pos_t[:, 0, :], 9, 9, ALU.logical_shift_right, ALU.logical_shift_left))
            link(V.tensor_scalar(pos_t[:, 2, :], pos_t[:, 0, :], 127, 2, ALU.bitwise_and, ALU.logical_shift_left))
            link(V.tensor_scalar(pos_t[:, 3, :], pos_t[:, 0, :], 7, 3, ALU.logical_shift_right, ALU.bitwise_and))
            link(V.tensor_tensor(pos_t[:, 4, :], pos_t[:, 1, :], pos_t[:, 2, :], ALU.bitwise_or))
            V.tensor_tensor(pos[:], pos_t[:, 4, :], pos_t[:, 3, :], ALU.bitwise_or).then_inc(S["pos_ok"], 1)
            dve.wait_ge(S["trowed"], 1)
            V.tensor_copy(trow[:], bank[7][0:1, 0:256]).then_inc(S["trow_ok"], 1)
            dve.wait_ge(S["w1_h"], 4)
            V.tensor_tensor(w1_l[:], w1_f, w1_h[:].bitcast(F32), ALU.subtract).then_inc(S["w_ok"], 1)
            V.tensor_tensor(wg_l[:], wg_f[:], wg_h[:].bitcast(F32), ALU.subtract).then_inc(S["w_ok"], 1)
            V.tensor_tensor(b2_r[32:33, :], b2_f[32:33, :], b2_r[32:33, :].bitcast(F32), ALU.subtract).then_inc(S["w_ok"], 1)
            for hh in range(2):
                r = slice(64 * hh, 64 * hh + 64)
                V.tensor_tensor(vo_blk[r, :, hh, :], vo_blk[r, :, hh, :], vo_row0[r, :, :], ALU.subtract).then_inc(S["w_ok"], 1)
            V.tensor_scalar(gi[:], ramp_f[:, 0:NE], 1000.0, None, ALU.add).then_inc(S["w_ok"], 1)
            for g in range(NG):
                dve.wait_ge(S["y_ps"], g + 1)
                if g >= 4:
                    dve.wait_ge(y_out_sem[g % 4], 16 * (g // 4))
                V.tensor_copy(y_out[:, g % 4, :], bank[2 + g % 2][:, 0:GT * D]).then_inc(S["y_ok"], 1)
            dve.wait_ge(S["scattered"], 16 * NC)

            def layernorm(b, done):
                if done == "xn_ready":
                    dve.wait_ge(S["y_loaded"], 16 * J * (b + 1))
                else:
                    dve.wait_ge(S["h1_ready"], J * (b + 1))
                h4 = hbuf[:, b * J:(b + 1) * J, :]
                wide = [128, J, D]
                s_ = [ln_s[:, i, :] for i in range(8)]
                link(V.tensor_reduce(s_[0], h4, AX.X, ALU.add))
                link(V.tensor_scalar(s_[1], s_[0], 1.0 / D, None, ALU.mult))
                yield
                link(V.tensor_tensor(ln_c[:], h4, s_[1].unsqueeze(2).to_broadcast(wide), ALU.subtract))
                yield
                link(V.tensor_tensor(ln_q[:], ln_c[:], ln_c[:], ALU.mult))
                yield
                link(V.tensor_reduce(s_[2], ln_q[:], AX.X, ALU.add))
                link(V.tensor_scalar(s_[3], s_[2], 1.0 / D, EPS, ALU.mult, ALU.add))
                link(V.tensor_scalar(s_[4].bitcast(I32), s_[3].bitcast(I32), 1, None, ALU.logical_shift_right))
                yield
                link(V.tensor_scalar(s_[5].bitcast(I32), s_[4].bitcast(I32), -1.0, float(0x5F3759DF), ALU.mult, ALU.add))
                for i in range(4):
                    if i == 2:
                        yield
                    link(V.scalar_tensor_tensor(s_[6], s_[5], -0.5, s_[5], ALU.mult, ALU.mult))
                    link(V.tensor_tensor(s_[7], s_[6], s_[3], ALU.mult))
                    link(V.scalar_tensor_tensor(s_[5], s_[7], 1.5, s_[5], ALU.add, ALU.mult))
                yield
                V.tensor_tensor(xn[:, b * J:(b + 1) * J, :, :], ln_c[:].unsqueeze(2).to_broadcast([128, J, 2, D]),
                                s_[5].unsqueeze(2).unsqueeze(3).to_broadcast([128, J, 2, D]), ALU.mult).then_inc(S[done], 1)

            def gate(b, logits):
                dve.wait_ge(S["gate_ps"], b + 1)
                l, eq, cand, oh1, l2, oh2, t1, t2 = (gt[:, i, :, :] for i in range(8))
                m1, i1, m2, i2, dd, ee, w1_, w2_ = (gs[:, i, :] for i in range(8))
                w3 = [128, J, NE]
                ramp3 = ramp_f[:, 0:NE].unsqueeze(1).to_broadcast(w3)
                gi3 = gi[:].unsqueeze(1).to_broadcast(w3)

                def over_e(v):
                    return v.unsqueeze(2).to_broadcast(w3)

                V.tensor_tensor(l, logits[:, 0:J * NE].rearrange("p (j e) -> p j e", e=NE),
                                bg_f[:, 0, :].unsqueeze(1).to_broadcast(w3), ALU.add).then_inc(S["gate_used"], 1)
                dve.wait_ge(S["gate_used"], b + 1)
                yield
                link(V.tensor_tensor(l, l, bg_f[:, 1, :].unsqueeze(1).to_broadcast(w3), ALU.add))

                def pick(l_, m_, i_, oh_):
                    link(V.tensor_reduce(m_, l_, AX.X, ALU.max))
                    link(V.tensor_tensor(eq, l_, over_e(m_), ALU.is_equal))
                    yield
                    link(V.scalar_tensor_tensor(cand, eq, -1000.0, gi3, ALU.mult, ALU.add))
                    link(V.tensor_reduce(i_, cand, AX.X, ALU.min))
                    link(V.tensor_tensor(oh_, ramp3, over_e(i_), ALU.is_equal))

                yield from pick(l, m1, i1, oh1)
                yield
                link(V.scalar_tensor_tensor(l2, oh1, -3.0e38, l, ALU.mult, ALU.add))
                yield from pick(l2, m2, i2, oh2)
                V.tensor_tensor(dd, m2, m1, ALU.subtract).then_inc(S["gd_ready"], 1)
                yield
                dve.wait_ge(S["ge_ready"], b + 1)
                link(V.tensor_scalar(w2_, ee, 1.0, None, ALU.add))
                link(V.reciprocal(w1_, w2_))
                link(V.tensor_tensor(w2_, ee, w1_, ALU.mult))
                link(V.tensor_tensor(t1, oh1, over_e(w1_), ALU.mult))
                link(V.tensor_tensor(t2, oh2, over_e(w2_), ALU.mult))
                link(V.tensor_tensor(comb[:], t1, t2, ALU.add))

            gating = iter(())
            for b in range(-2, B + 3):
                if b == -2:
                    for _ in layernorm(0, "xn_ready"):
                        pass
                parts = iter(())
                for k in range(16):
                    if k == 0 and 0 <= b - 2 < B:
                        parts = layernorm(b - 2, "xn2_ready")
                    if k == 8 and b + 3 < B:
                        parts = layernorm(b + 3, "xn_ready")
                    next(parts, None)
                    if k == 0 or 9 <= k <= 12:
                        next(gating, None)
                    for u in s_units(b, k):
                        nb = b + 1
                        n = 32 * nb + u
                        dve.wait_ge(S["s_ps"], n + 1)
                        if nb >= 1 and u % 16 == 0:
                            dve.wait_ge(S["mt_ps"], 2 * nb - 1 + u // 16)
                        V.tensor_reduce(mx[:, u // 16, u % 16:u % 16 + 1], bank[3 + n % 2][:], AX.X, ALU.max).then_inc(S["mx_done"], 1)
                    for a in aux_at(b, k):
                        kind, ab, i = a
                        if kind == "xT":
                            dve.wait_ge(S["x_hi"], ab + 1)
                            lo_rows = xs[64:128, 0, :]
                            V.tensor_tensor(lo_rows, ring(a)[64:128, :], lo_rows.bitcast(F32), ALU.subtract).then_inc(S["xs_ready"], 1)
                        if kind == "xT2":
                            dve.wait_ge(S["x2_hi"], ab + 1)
                            lo_rows = xs[64:128, 1, :]
                            V.tensor_tensor(lo_rows, ring(a)[64:128, :], lo_rows.bitcast(F32), ALU.subtract).then_inc(S["xs2_ready"], 1)
                        if kind == "gate":
                            gating = gate(ab, ring(a))
                            next(gating)
                        if kind == "down":
                            dve.wait_ge(S["dn_ps"], J * ab + i + 1)
                            folded(dve, a)
                            V.tensor_tensor(vtmp[:, term[a] % 2, :].rearrange("p (e d) -> p e d", d=D),
                                            ring(a)[:].rearrange("p (e d) -> p e d", d=D),
                                            comb[:, i, :].unsqueeze(2).to_broadcast([128, NE, D]), ALU.mult).then_inc(S["dn_used"], 1)
                        if kind == "proj":
                            dve.wait_ge(S["qk_hi"], 4 * ab + i + 1)
                            V.tensor_tensor(qk_l[:, i, :], ring(a)[:], qk_h[:, i, :].bitcast(F32), ALU.subtract).then_inc(S["qk_lo"], 1)
                        if kind == "rt":
                            dve.wait_ge(S["rt_ps"], ab + 1)
                            if ab >= 1:
                                dve.wait_ge(S["vo_used"], J * ab)
                            V.reciprocal(rsum[:].rearrange("p j t q -> p (j t q)"), ring(a)[:, 0:8 * J]).then_inc(S["rsum_ready"], 1)
                        if kind == "vo":
                            n = J * ab + i
                            dve.wait_ge(S["vo_ps"], n + 1)
                            dve.wait_ge(S["rsum_ready"], ab + 1)
                            folded(dve, a)
                            V.tensor_tensor(vtmp[:, term[a] % 2, :].rearrange("p (q t e) -> p t q e", t=2, e=D),
                                            ring(a)[:].rearrange("p (q t e) -> p t q e", t=2, e=D),
                                            rsum[:, i, :, :].unsqueeze(3).to_broadcast([128, 2, NPAIR, D]),
                                            ALU.mult).then_inc(S["vo_used"], 1)

        @block.tensor
        def _(pe):
            M = nc.tensor.matmul
            pe.wait_ge(S["ohT_ok"], 1)
            pe.wait_ge(S["tab_ok"], 1)
            cols = ohT[:].rearrange("h (p c) -> h c p", c=NC)
            per = 512 // LO
            for c in range(NC):
                last = M(bank[c // per][:, c % per * LO:(c % per + 1) * LO], cols[:, c, :], tab[:], start=True, stop=True)
                if c % per == per - 1:
                    last.then_inc(S["looked"], 1)
            pe.wait_ge(S["qk_in"], 16 * 8)
            pe.wait_ge(S["cst_in"], 16)
            for o in range(4):
                last = nc.tensor.transpose(bank[7][:, o * 128:(o + 1) * 128], qk_nat[:, o, :, :].rearrange("p t d -> p (t d)"), ident)
            last.then_inc(S["wq_ps"], 1)
            pe.wait_ge(S["run_ok"], 1)
            pe.wait_ge(S["cons_ok"], 3)
            for q in range(NCH):
                w = min(CB, NC - q * CB)
                M(bank[q][:, 0:w * NR], upper[:], oh[:, q * CB:q * CB + w, :], start=True, stop=False)
                M(bank[q][:, 0:w * NR], ones_bf[:], run[:, q * CB:q * CB + w, :], start=False, stop=False)
            pe.wait_ge(S["wq_ok"], 1)
            M(bank[7][:, 0:NR], ones_bf[:], run[:, NC, :], start=True, stop=True).then_inc(S["ranked"], 1)
            pe.wait_ge(S["tb_ok"], 1)
            for q in range(NCH):
                w = min(CB, NC - q * CB)
                last = M(bank[q][:, 0:w * NR], ctile_bf[:], tbase[:].unsqueeze(1).to_broadcast([1, w, NR]), start=False, stop=True)
            last.then_inc(S["placed"], 1)
            pe.wait_ge(S["trule_ok"], 1)
            for i in range(2):
                last = M(bank[7][0:1, i * 128:(i + 1) * 128], trule[:, i:i + 1], ident, start=True, stop=True)
            last.then_inc(S["trowed"], 1)
            pe.wait_ge(S["trow_ok"], 1)
            pe.wait_ge(S["rules_in"], 16)
            for g in range(NG + 1):
                if g < NG:
                    at_next = nc.values_load_multi_w_load_instructions(
                        trow[0:1, g * GT:(g + 1) * GT], engines=[mybir.EngineType.PE], min_val=0, max_val=(NR - 1) * D,
                        skip_runtime_bounds_check_because="clamped above")[1]
                    pe.wait_ge(e_in_sem[g % NE_IN], 16 * (g // NE_IN + 1))
                    if g >= 2:
                        pe.wait_ge(S["eT_ok"], g - 1)
                    for i in range(GT // 2):
                        last = nc.tensor.transpose(bank[g % 2][:, i * 128:(i + 1) * 128],
                                                   e_in[:, g % NE_IN, 2 * i * D:2 * (i + 1) * D], ident)
                    last.then_inc(S["eT_ps"], 1)
                if g >= 1:
                    q = g - 1
                    pe.wait_ge(S["eT_ok"], q + 1)
                    if q >= 2:
                        pe.wait_ge(S["y_ok"], q - 1)
                    for s in range(GT):
                        col = s % 2 * 256 + s // 2 * 128
                        last = M(bank[2 + q % 2][:, s * D:(s + 1) * D], eT[:, q % 2, col:col + TS],
                                 r_sb[:, bass.ds(at[s], D)], start=True, stop=True)
                    last.then_inc(S["y_ps"], 1)
                at = at_next

            pe.wait_ge(S["wq_ok"], 1)
            pe.wait_ge(S["w_ok"], 6)

            def aux(a):
                kind, b, i = a
                out_ = ring(a)
                if kind == "xT":
                    pe.wait_ge(S["xn_ready"], b + 1)
                if kind == "xT2":
                    pe.wait_ge(S["xn2_ready"], b + 1)
                drained(pe, a)
                if kind in ("xT", "xT2"):
                    for j in range(J):
                        last = nc.tensor.transpose(out_[:, j * 128:(j + 1) * 128],
                                                   xn[:, b * J + j, :, :].rearrange("p t d -> p (t d)"), ident)
                    last.then_inc(S[kind + "_ps"], 1)
                if kind == "proj":
                    pe.wait_ge(S["xs_ready"], b + 1)
                    M(out_[:], wqk_h[:, i, :], xs[:, 0, :], start=True, stop=False)
                    M(out_[:], wqk_l[:, i, :], xs[:, 0, :], start=False, stop=True).then_inc(S["proj_ps"], 1)
                if kind == "gate":
                    pe.wait_ge(S["xs2_ready"], b + 1)
                    for j in range(J):
                        o = out_[:, j * NE:(j + 1) * NE]
                        M(o, xs[:, 1, j * 128:(j + 1) * 128], wg_h[:], start=True, stop=False)
                        last = M(o, xs[:, 1, j * 128:(j + 1) * 128], wg_l[:], start=False, stop=True)
                    last.then_inc(S["gate_ps"], 1)
                if kind == "up":
                    M(out_[:], w1_h[:, i * HID:(i + 1) * HID], xs[:, 1, :], start=True, stop=False)
                    M(out_[:], w1_l[:, i * HID:(i + 1) * HID], xs[:, 1, :], start=False, stop=True).then_inc(S["up_ps"], 1)
                if kind == "down":
                    pe.wait_ge(S["relu_done"], NE * (b + 1))
                    M(out_[:], ones_r[:], b2_r[:], start=True, stop=False)
                    for e in range(NE):
                        last = M(out_[:, e * D:(e + 1) * D], hid[:, e, i * 128:(i + 1) * 128], w2_f[:, e, :],
                                 start=False, stop=(e == NE - 1))
                    last.then_inc(S["dn_ps"], 1)
                if kind == "mt":
                    pe.wait_ge(S["mx_done"], 32 * b + 16 * (i + 1))
                    nc.tensor.transpose(out_[0:4 * J, 0:128], mx[:, i, :], ident).then_inc(S["mt_ps"], 1)
                if kind == "rt":
                    pe.wait_ge(S["srow_in"], 32 * (b + 1))
                    for j in range(J):
                        last = nc.tensor.transpose(out_[:, j * 8:(j + 1) * 8], srow[:, j * 128:(j + 1) * 128], ident[0:8, 0:8])
                    last.then_inc(S["rt_ps"], 1)
                if kind == "vo":
                    pe.wait_ge(S["ctx_copied"], NPAIR * (b + 1))
                    for pair in range(NPAIR):
                        last = M(out_[:, pair * 128:(pair + 1) * 128], ctxT[:, b % 2, pair, i * 128:(i + 1) * 128],
                                 vo_blk[:, pair, :, :].rearrange("p t e -> p (t e)"), start=True, stop=True)
                    last.then_inc(S["vo_ps"], 1)

            for b in range(-2, B + 3):
                for k in range(16):
                    step = 16 * b + k + 1
                    for u in (2 * step, 2 * step + 1):
                        if 0 <= u < 32 * B:
                            ub, pair, ut, hh = u // 32, u // 8 % 4, u // 2 % 4, u % 2
                            h = 2 * pair + hh
                            pe.wait_ge(S["m_in"], 32 * ub + 16 * (h // 4 + 1))
                            if u >= NST:
                                pe.wait_ge(S["exp_done"], u - NST + 1)
                            M(bank[u % NST][:], ks[:, ub % 2, h, ut * 128:(ut + 1) * 128], qs[:, ub % 2, h, :],
                              start=True, stop=True).then_inc(S["st_ps"], 1)
                    todo = list(s_units(b, k))

                    def score_tile():
                        if not todo:
                            return
                        u = todo.pop(0)
                        nb = b + 1
                        n = 32 * nb + u
                        h, tt = u // J, u % J
                        pe.wait_ge(S[f"stack_{h // 2}"], 96 * (nb + 1))
                        if n >= 2:
                            pe.wait_ge(S["mx_done"], n - 1)
                        M(bank[3 + n % 2][:], qs[0:96, nb % 2, h, tt * 128:(tt + 1) * 128], ks[0:96, nb % 2, h, :],
                          start=True, stop=True).then_inc(S["s_ps"], 1)

                    score_tile()
                    if 0 <= b < B:
                        pair, ut = k // 4, k % 4
                        pe.wait_ge(S["exp_done"], 32 * b + 2 * k + 2)
                        pe.wait_ge(S["xa_ready"], b + 1)
                        if ut == 0 and NPAIR * b + pair >= 1:
                            pe.wait_ge(S["ctx_copied"], NPAIR * b + pair)
                        for hh in range(2):
                            last = M(bank[5][64 * hh:64 * hh + 64, :], xa[:, b * J + ut, :],
                                     prob[:, (16 * b + k) % NPROB, hh, :], start=(ut == 0), stop=(ut == J - 1))
                        last.then_inc(S["pv_done"], 1)
                    score_tile()
                    for a in aux_at(b, k):
                        aux(a)
                    score_tile()


INPUTS = ['x', 'L0_tok_base_embeddings', 'L0_tok_rule_transform', 'L0_tok_token_rules', 'L0_attn_Q', 'L0_attn_K',
          'L0_attn_VO', 'L0_ffn_Wg', 'L0_ffn_bg', 'L0_ffn_bias', 'L0_ffn_W1', 'L0_ffn_b1', 'L0_ffn_W2', 'L0_ffn_b2']


def kernel(**inputs):
    import concourse.bacc as bacc
    from concourse.bass_utils import run_bass_kernel_spmd

    nc = bacc.Bacc("TRN2", target_bir_lowering=False, num_devices=1)
    arrays = {f"in_{name}": np.ascontiguousarray(inputs[name]) for name in INPUTS}
    arrays["in_consts"] = shape_constants()
    args = [nc.dram_tensor(name, a.shape, mybir.dt.from_np(a.dtype), kind="ExternalInput").ap() for name, a in arrays.items()]
    batch, seq = inputs["x"].shape
    width = inputs["L0_tok_base_embeddings"].shape[1]
    out = nc.dram_tensor("out", (batch, seq, width), mybir.dt.float32, kind="ExternalOutput").ap()
    lm_tower_kernel(nc, *args, out)
    return run_bass_kernel_spmd(nc, [arrays], core_ids=[0]).results[0]["out"]
```

```python
from contextlib import ExitStack

import numpy as np
import concourse.bass as bass
from concourse import mybir


def shape_constants():
    p = np.arange(128)
    eye = np.eye(128)
    minus_lower = -(p[:, None] >= p[None, :]).astype(np.float64)
    ramp = np.broadcast_to(p[None, :], (128, 128))
    cols = np.stack([p, p + 128], axis=1)
    not_first = np.broadcast_to(p[None, :32] > 0, (128, 32))
    return np.concatenate([eye, minus_lower, ramp, cols, not_first], axis=1).astype(np.float32)


def lm_tower_kernel(nc, x, base_emb, rule_tr, tok_rules, Q, K, VO, Wg, bg, gbias, W1, b1, W2, b2, consts, out):
    F32, F32R, BF16, I32 = mybir.dt.float32, mybir.dt.float32r, mybir.dt.bfloat16, mybir.dt.int32
    ALU, ACT, AX = mybir.AluOpType, mybir.ActivationFunctionType, mybir.AxisListType

    B, T = x.shape
    VOCAB, D = base_emb.shape
    NR = rule_tr.shape[0]
    H, R, _ = Q.shape
    NE, _, HID = W1.shape
    J = T // 128
    NC = B * J
    LO = 64
    HI = VOCAB // LO
    TS = 128
    GT = 4
    MAXT = (B * T + NR * (TS - 1)) // TS
    NG = -(-MAXT // GT)
    NE_IN = 8
    WARM = 10
    NPAIR = H // 2
    EPS = 1e-5
    SC = 1.0 / float(D) ** 0.5
    CB = 5
    NCH = -(-NC // CB)

    ctx = ExitStack()
    with ctx:
        def sb(name, shape, dt=F32):
            return ctx.enter_context(nc.sbuf_tensor(name, shape, dt))

        def sem(name):
            return ctx.enter_context(nc.semaphore(name))

        bank = [ctx.enter_context(nc.psum_tensor(f"bank{i}", [128, 512], F32)) for i in range(8)]
        emb_sorted = nc.dram_tensor("emb_sorted", (NG * GT * 128, D), F32, kind="Internal").ap()
        y_sorted = nc.dram_tensor("y_sorted", (NG * GT * 128, D), F32, kind="Internal").ap()
        hi_dram = nc.dram_tensor("hi_dram", (128, NC), BF16, kind="Internal").ap()

        NPROB = 4
        cst = sb("cst", [128, 386 + NC])
        not_first = cst[:, 386:386 + NC]
        ident, minus_lower_f, ramp_f, part_f = cst[:, 0:128], cst[:, 128:256], cst[:, 256:384], cst[:, 384:386]
        minus_lower = sb("minus_lower", [128, 128], BF16)
        ones_bf = sb("ones_bf", [128, 128], BF16)
        ctile_bf = sb("ctile_bf", [1, 128], BF16)
        qk_nat = sb("qk_nat", [128, 4, 2, D])
        wqk_h = sb("wqk_h", [128, 4, 128], F32R)
        wqk_l = sb("wqk_l", [128, 4, 128], F32R)
        vo_blk = sb("vo_blk", [128, NPAIR, 2, D])
        vo_row0 = sb("vo_row0", [128, NPAIR, D])
        vtmp = sb("vtmp", [128, 2, 8 * D])
        w1_f = vtmp[:].rearrange("p a n -> p (a n)")
        w1_h = sb("w1_h", [128, NE * HID], F32R)
        w1_l = sb("w1_l", [128, NE * HID], F32R)
        w2_f = sb("w2_f", [HID, NE, D])
        b1_f = sb("b1_f", [HID, NE])
        wg_f = sb("wg_f", [128, NE])
        wg_h = sb("wg_h", [128, NE], F32R)
        wg_l = sb("wg_l", [128, NE], F32R)
        bg_f = sb("bg_f", [128, 2, NE])
        b2_f = sb("b2_f", [128, NE // 2])
        ones_r = sb("ones_r", [32, 128], F32R)
        ones_f = sb("ones_f", [128, 128])
        hbuf = sb("hbuf", [128, NC, D])
        xn = sb("xn", [128, NC, 2, D])
        xa = sb("xa", [128, NC, D])
        pos = sb("pos", [128, NC], I32)
        mark = sb("mark", [1, 1])
        xs = sb("xs", [128, 2, 512], F32R)
        qk_h = sb("qk_h", [128, 4, 512], F32R)
        qk_l = sb("qk_l", [128, 4, 512], F32R)
        mx = sb("mx", [128, 2, 4 * J])
        negm = sb("negm", [4 * J, 2, 128], F32R)
        ctxT = sb("ctxT", [128, 2, NPAIR, 512])
        srow = sb("srow", [8, 512])
        rsum = sb("rsum", [128, J, 2, NPAIR])
        acc = sb("acc", [128, 2, 8 * D])
        ln_c = sb("ln_c", [128, J, D])
        ln_q = sb("ln_q", [128, J, D])
        ln_s = sb("ln_s", [128, 8, J])
        gt = sb("gt", [128, 8, J, NE])
        gs = sb("gs", [128, 8, J])
        gi = sb("gi", [128, NE])
        comb = sb("comb", [128, J, NE])
        hid = sb("hid", [HID, NE, 512])

        with ExitStack() as part:
            def tb(name, shape, dt=F32):
                return part.enter_context(nc.sbuf_tensor(name, shape, dt))

            ids = tb("ids", [128, 4, NC], I32)
            idf = tb("idf", [128, 3, NC])
            hi_bf = tb("hi_bf", [128, NC], BF16)
            hi_b = tb("hi_b", [HI, 128 * NC], BF16)
            ohT = tb("ohT", [HI, 128 * NC], BF16)
            tab_i = tb("tab_i", [HI, LO], I32)
            tab_f = tb("tab_f", [HI, 2, LO])
            tab = tb("tab", [HI, LO], BF16)
            oh_lo = tb("oh_lo", [128, NC, LO])
            rule = tb("rule", [128, NC])
            oh = tb("oh", [128, NR, NC], BF16)
            run = tb("run", [128, NR, NC], BF16)
            again = qk_l[:].rearrange("p a n -> p (a n)").bitcast(BF16)[:, 0:NR * NC].rearrange("p (r c) -> p r c", c=NC)
            sel = ctxT[:].rearrange("p a q t -> p (a q t)")[:, 0:NC * NR].rearrange("p (c r) -> p c r", r=NR)
            cnt = tb("cnt", [128, 4, NR])
            cnt_i = tb("cnt_i", [128, 2, NR], I32)
            tbase = tb("tbase", [1, NR], BF16)
            zero_nr = tb("zero_nr", [128, NR])
            trule = tb("trule", [128, 2])
            trow = tb("trow", [1, 256], I32)
            pos_t = tb("pos_t", [128, 5, NC], I32)
            etok = xn[:, :, 0, :]
            zrow = tb("zrow", [128, NG * GT * D // 4])
            r_sb = tb("r_sb", [D, NR * D])
            flat_hid = hid[:].rearrange("p e n -> p (e n)")
            e_in = flat_hid[:, 0:NE_IN * GT * D].rearrange("p (g n) -> p g n", g=NE_IN)
            y_out = flat_hid[:, NE_IN * GT * D:(NE_IN + 4) * GT * D].rearrange("p (g n) -> p g n", g=4)
            eT = tb("eT", [D, 2, 512])
        with ExitStack() as part:
            qs = part.enter_context(nc.sbuf_tensor("qs", [97, 2, H, 512], F32R))
            ks = part.enter_context(nc.sbuf_tensor("ks", [97, 2, H, 512], F32R))
            prob = part.enter_context(nc.sbuf_tensor("prob", [128, NPROB, 2, 512], F32))
        
        names = """again_ok scatters_issued xa_set xn2_ready stack_0 stack_1 stack_2 stack_3 cst_in ids_in tab_in
            rules_in qk_in w_in zero_set zeroed ids_ok hi_ok hi_out hi_in ohT_ok tab_ok looked
            run_ok cons_ok ranked tb_ok placed pos_ok trule_ok trowed trow_ok e_got scattered eT_ps
            eT_ok y_ps y_ok xn_ready xa_ready wq_ps wq_h wq_ok w1_h b_set w_ok xT_ps x_hi xs_ready
            xT2_ps x2_hi xs2_ready proj_ps qk_hi qk_lo ks_one s_ps mx_done mt_ps negm_ready m_in
            st_ps exp_done pv_done ctx_copied srow_in rt_ps rsum_ready vo_ps vo_used h1_ready
            gate_ps gate_used gd_ready ge_ready up_ps relu_done dn_ps dn_ok bk_ps bk_used h2_ready
            out_done dve_chain pool_chain""".split()
        S = {n: sem(n) for n in names}
        e_in_sem = [sem(f"e_in{i}") for i in range(NE_IN)]
        y_loaded = [sem(f"y_loaded{b}") for b in range(B)]
        y_out_sem = [sem(f"y_out{i}") for i in range(4)]

        RING = 2

        XT, PROJ, MT, RT, VO_STEPS = 4, (5, 6, 7, 8), (9, 1), 6, (9, 11, 13, 14)
        XT2, GATE, UP, DOWN, BACK = 7, 8, (9, 10, 11, 12, 13, 14, 15, 15), (12, 15, 15), (1, 2, 3, 4)

        def last_products(k):
            def down(b):
                return [("down", b, p) for p in range(NE // 2)]

            def back(b, tiles):
                return [("back", b, j) for j in tiles]

            def up(b, experts):
                return [("up", b, e) for e in experts]

            def vo(i):
                return [("vo", B - 1, i)]

            return {0: [("down", B - 3, 3), ("xT2", B - 2, 0)],
                    1: back(B - 3, (0, 1)) + [("gate", B - 2, 0)],
                    2: back(B - 3, (2, 3)) + [("rt", B - 1, 0)],
                    3: up(B - 2, (0,)) + vo(0) + up(B - 2, (1,)),
                    4: vo(1) + up(B - 2, (2, 3)),
                    5: vo(2) + up(B - 2, (4,)),
                    6: vo(3) + up(B - 2, (5,)),
                    7: up(B - 2, (6, 7)),
                    8: down(B - 2) + back(B - 2, (0, 1)),
                    9: back(B - 2, (2, 3)),
                    10: [("xT2", B - 1, 0), ("gate", B - 1, 0)],
                    11: up(B - 1, (0, 1)), 12: up(B - 1, (2, 3)), 13: up(B - 1, (4, 5)), 14: up(B - 1, (6, 7)),
                    15: down(B - 1) + back(B - 1, range(J))}[k]

        def aux_at(b, k):
            todo = []
            if b == B:
                return last_products(k)
            if k == 0 and 0 <= b - 3 < B:
                todo.append(("down", b - 3, 3))
            if k == MT[1] and 0 <= b < B:
                todo.append(("mt", b, 1))
            if k in BACK and 0 <= b - 3 < B:
                todo.append(("back", b - 3, BACK.index(k)))
            if k == XT and 0 <= b + 2 < B:
                todo.append(("xT", b + 2, 0))
            if k in PROJ and 0 <= b + 2 < B:
                todo.append(("proj", b + 2, PROJ.index(k)))
            if k == XT2 and 0 <= b - 2 < B:
                todo.append(("xT2", b - 2, 0))
            if k == RT and 0 <= b - 1 < B:
                todo.append(("rt", b - 1, 0))
            if k == GATE and 0 <= b - 2 < B:
                todo.append(("gate", b - 2, 0))
            if k == MT[0] and 0 <= b + 1 < B:
                todo.append(("mt", b + 1, 0))
            if k in VO_STEPS and 0 <= b - 1 < B:
                todo.append(("vo", b - 1, VO_STEPS.index(k)))
            if 0 <= b - 2 < B:
                todo += [("up", b - 2, e) for e in range(NE) if UP[e] == k]
                todo += [("down", b - 2, p) for p in range(3) if DOWN[p] == k]
            return todo

        order = [a for b in range(-2, B + 1) for k in range(16) for a in aux_at(b, k)]
        slot = {a: n for n, a in enumerate(order)}

        def ring(a):
            return bank[6 + slot[a] % RING]

        def drained(eng, a):
            n = slot[a] - RING
            if n < 0:
                return
            kind, b, i = order[n]
            if kind == "mt":
                eng.wait_ge(S["negm_ready"], 2 * b + i + 1)
            if kind == "rt":
                eng.wait_ge(S["rsum_ready"], b + 1)
            if kind == "vo":
                eng.wait_ge(S["vo_used"], J * b + i + 1)
            if kind == "xT":
                eng.wait_ge(S["xs_ready"], b + 1)
            if kind == "proj":
                eng.wait_ge(S["qk_lo"], 4 * b + i + 1)
            if kind == "xT2":
                eng.wait_ge(S["xs2_ready"], b + 1)
            if kind == "gate":
                eng.wait_ge(S["gate_used"], b + 1)
            if kind == "up":
                eng.wait_ge(S["relu_done"], NE * b + i + 1)
            if kind == "down":
                eng.wait_ge(S["dn_ok"], NE // 2 * b + i + 1)
            if kind == "back":
                eng.wait_ge(S["bk_used"], J * b + i + 1)

        sums = [a for a in order if a[0] in ("vo", "back")]
        term = {a: n for n, a in enumerate(sums)}

        def folded(eng, a):
            if term[a] >= 2:
                kind, b, i = sums[term[a] - 2]
                eng.wait_ge(S["h1_ready" if kind == "vo" else "h2_ready"], J * b + i + 1)

        def s_units(b, k):
            if not 0 <= b + 1 < B:
                return []
            return range(2 * k, 2 * k + 2)

        gate_exps = [(b + 2, 15) for b in range(B - 2)] + [(B, 5), (B, 14)]

        NST = 3
        block = ctx.enter_context(nc.Block())

        @block.sync
        def _(sp):
            sp.dma_start(ids[:, 0, :].rearrange("p (b j) -> p b j", j=J), x.rearrange("b (p j) -> p b j", j=J)).then_inc(S["ids_in"], 16)
            sp.dma_start(tab_i[:], tok_rules.rearrange("(h l) -> h l", l=LO)).then_inc(S["tab_in"], 16)
            sp.dma_start(cst[:], consts).then_inc(S["cst_in"], 16)
            sp.wait_ge(S["hi_ok"], 1)
            sp.dma_start(hi_dram, hi_bf[:]).then_inc(S["hi_out"], 16)
            sp.wait_ge(S["hi_out"], 16)
            sp.dma_start(hi_b[:], hi_dram.rearrange("p c -> (p c)").partition_broadcast(HI)).then_inc(S["hi_in"], 16)
            sp.dma_start(r_sb[:].rearrange("d (r e) -> d r e", e=D), rule_tr.rearrange("r d e -> d r e")).then_inc(S["rules_in"], 16)
            es = emb_sorted.rearrange("(g p s) d -> g p (s d)", p=128, s=GT)
            ys = y_sorted.rearrange("(g p s) d -> g p (s d)", p=128, s=GT)
            sp.wait_ge(S["w1_h"], 3)
            sp.wait_ge(S["scattered"], 16 * NC)
            for g in range(NG + NE_IN - 2):
                if g < NG:
                    if g >= NE_IN:
                        sp.wait_ge(S["eT_ps"], g - NE_IN + 1)
                    sp.dma_start(e_in[:, g % NE_IN, :], es[g]).then_inc(e_in_sem[g % NE_IN], 16)
                if g >= NE_IN - 2:
                    q = g - NE_IN + 2
                    sp.wait_ge(S["y_ok"], q + 1)
                    sp.dma_start(ys[q], y_out[:, q % 4, :]).then_inc(y_out_sem[q % 4], 16)
            for i in range(2):
                sp.dma_start(ks[96:97, i, :, :].rearrange("o h (t n) -> o (h t) n", n=128).bitcast(F32),
                             ones_r[0:32, :].bitcast(F32)).then_inc(S["ks_one"], 16)
            def stack(b, g):
                if g == 0:
                    sp.wait_ge(S["qk_lo"], 4 * b + 4)
                if b >= 2:
                    sp.wait_ge(S["exp_done"], 32 * (b - 2) + 8 * (g + 1))
                for dst, o, parts in ((qs, 0, (qk_h, qk_l, qk_h)), (ks, 2, (qk_h, qk_h, qk_l))):
                    for s, src in enumerate(parts):
                        sp.dma_start(dst[32 * s:32 * s + 32, b % 2, 2 * g:2 * g + 2, :].bitcast(F32),
                                     src[32 * g:32 * g + 32, o:o + 2, :].bitcast(F32)).then_inc(S[f"stack_{g}"], 16)

            def max_row(b, half):
                sp.wait_ge(S["negm_ready"], 2 * b + half + 1)
                sp.dma_start(qs[96:97, b % 2, 4 * half:4 * half + 4, :].rearrange("o h (t n) -> o (h t) n", n=128).bitcast(F32),
                             negm[:, half, :].bitcast(F32)).then_inc(S["m_in"], 16)
                sp.wait_ge(S["m_in"], 32 * b + 16 * half + 16)

            for b in range(-2, B + 1):
                if 0 <= b - 1 < B:
                    sp.wait_ge(S["ctx_copied"], NPAIR * b)
                    if b >= 2:
                        sp.wait_ge(S["rt_ps"], b - 1)
                    for hh in range(2):
                        sp.dma_start(srow[4 * hh:4 * hh + 4, :], ctxT[64 * hh:64 * hh + 1, (b - 1) % 2, :, :]).then_inc(S["srow_in"], 16)
                    sp.wait_ge(S["srow_in"], 32 * b)
                if 0 <= b < B:
                    max_row(b, 1)
                if 0 <= b + 1 < B:
                    stack(b + 1, 3)
                if 0 <= b + 2 < B:
                    stack(b + 2, 0)
                    stack(b + 2, 1)
                if 0 <= b + 1 < B:
                    max_row(b + 1, 0)
                if 0 <= b + 2 < B:
                    stack(b + 2, 2)
                for done in range(B - 3, B) if b == B else range(b - 3, b - 2) if b >= 3 else ():
                    sp.wait_ge(S["h2_ready"], J * (done + 1))
                    sp.dma_start(out[done].rearrange("(p j) d -> p j d", j=J),
                                 hbuf[:, done * J:(done + 1) * J, :]).then_inc(S["out_done"], 16)
            sp.wait_ge(S["out_done"], 16 * B)

        @block.gpsimd
        def _(pool):
            pool.wait_ge(S["ids_ok"], 1)
            for c in range(NC):
                nc.gpsimd.indirect_dma_start(etok[:, c, :], None, base_emb,
                                             bass.IndirectOffsetOnAxis(ap=ids[:, 1, c:c + 1], axis=0)).then_inc(S["e_got"], 16)
            nc.gpsimd.memset(xa[:], 1.0).then_inc(S["xa_set"], 1)
            pool.wait_ge(S["xa_set"], 1)
            pool.wait_ge(S["e_got"], 16 * NC)
            pool.wait_ge(S["zeroed"], 16 * 4)
            pool.wait_ge(S["pos_ok"], 1)
            for c in range(NC):
                nc.gpsimd.indirect_dma_start(emb_sorted, bass.IndirectOffsetOnAxis(ap=pos[:, c:c + 1], axis=0),
                                             etok[:, c, :], None).then_inc(S["scattered"], 16)
            nc.gpsimd.memset(mark[:], 0.0).then_inc(S["scatters_issued"], 1)
            for q in range(4):
                pool.wait_ge(y_out_sem[q], 16 * len(range(q, NG, 4)))
            for b in range(B):
                for c in range(b * J, (b + 1) * J):
                    nc.gpsimd.indirect_dma_start(hbuf[:, c, :], None, y_sorted,
                                                 bass.IndirectOffsetOnAxis(ap=pos[:, c:c + 1], axis=0)).then_inc(y_loaded[b], 16)
            n = 0

            def fold(a_, done, ready):
                nonlocal n
                _, b, i = a_
                c = J * b + i
                pool.wait_ge(S[done], c + 1)
                v, a = vtmp[:, term[a_] % 2, :], acc[:, term[a_] % 2, :]
                src = v
                width = 4 * D
                at = 0
                while width >= D:
                    nc.gpsimd.tensor_tensor(a[:, at:at + width], src[:, 0:width], src[:, width:2 * width], ALU.add).then_inc(S["pool_chain"], 1)
                    n += 1
                    pool.wait_ge(S["pool_chain"], n)
                    src = a[:, at:at + width]
                    at += width
                    width //= 2
                nc.gpsimd.tensor_tensor(hbuf[:, c, :], hbuf[:, c, :], src, ALU.add).then_inc(S[ready], 1)

            for b in range(-2, B + 1):
                if b + 2 < B:
                    pool.wait_ge(S["xn_ready"], b + 3)
                    c = slice((b + 2) * J, (b + 3) * J)
                    nc.gpsimd.tensor_copy(xa[:, c, 1:D], xn[:, c, 0, 1:D]).then_inc(S["xa_ready"], 1)
                for k in range(16):
                    for a in aux_at(b, k):
                        if a[0] == "vo":
                            fold(a, "vo_used", "h1_ready")
                        if a[0] == "back":
                            fold(a, "bk_used", "h2_ready")

        @block.scalar
        def _(act):
            act.wait_ge(S["cst_in"], 16)
            nc.scalar.copy(again, not_first.unsqueeze(1).to_broadcast([128, NR, NC])).then_inc(S["again_ok"], 1)
            act.wait_ge(S["hi_in"], 16)
            act.wait_ge(S["zero_set"], 1)
            flat = emb_sorted.rearrange("(z p s) d -> z p (s d)", z=4, p=128)
            for i in range(4):
                act.dma_start(flat[i], zrow[:]).then_inc(S["zeroed"], 16)
            for i, src in enumerate((Q, K)):
                for half in range(2):
                    for dup in range(2):
                        act.dma_start(qk_nat[:, 2 * i + half, dup, :],
                                      src[4 * half:4 * half + 4].rearrange("h r d -> (h r) d")).then_inc(S["qk_in"], 16)
            act.wait_ge(S["b_set"], 2)
            for hh in range(2):
                act.dma_start(vo_blk[64 * hh:64 * hh + 64, :, hh, :],
                              VO.rearrange("(t q) d e -> t d q e", t=2)[hh]).then_inc(S["w_in"], 16)
                act.dma_start(vo_row0[64 * hh:64 * hh + 64, :, :],
                              VO.rearrange("(t q) d e -> t d q e", t=2)[hh, 0].partition_broadcast(64)).then_inc(S["w_in"], 16)
                act.dma_start(w1_f[64 * hh:64 * hh + 64, :].rearrange("d (e n) -> d e n", n=HID),
                              W1.rearrange("e d n -> d e n")).then_inc(S["w_in"], 16)
                act.dma_start(wg_f[64 * hh:64 * hh + 64, :], Wg).then_inc(S["w_in"], 16)
                with nc.allow_non_contiguous_dma(reason="one small transposed load"):
                    act.dma_start(b2_f[64 * hh:64 * hh + 64, :], b2.rearrange("(q t) d -> t d q", t=2)[hh]).then_inc(S["w_in"], 16)
            act.dma_start(w2_f[:], W2.rearrange("e n d -> n e d")).then_inc(S["w_in"], 16)
            act.dma_start(bg_f[:, 0, :], bg.partition_broadcast(128)).then_inc(S["w_in"], 16)
            act.dma_start(bg_f[:, 1, :], gbias.partition_broadcast(128)).then_inc(S["w_in"], 16)
            with nc.allow_non_contiguous_dma(reason="one small transposed load"):
                act.dma_start(b1_f[:], b1.rearrange("e n -> n e")).then_inc(S["w_in"], 16)
            act.wait_ge(S["wq_ps"], 1)
            nc.scalar.copy(wqk_h[:].rearrange("p o n -> p (o n)"), bank[7][:]).then_inc(S["wq_h"], 1)
            act.wait_ge(S["w_in"], 16 * 14)
            nc.scalar.copy(w1_h[:], w1_f).then_inc(S["w1_h"], 1)
            nc.scalar.copy(wg_h[:], wg_f[:]).then_inc(S["w1_h"], 1)
            nc.scalar.copy(ones_r[:], ones_f[0:32, :]).then_inc(S["w1_h"], 1)
            for g in range(NG):
                act.wait_ge(S["eT_ps"], g + 1)
                if g >= 2:
                    act.wait_ge(S["y_ps"], g - 1)
                for r in range(2):
                    ins = nc.scalar.copy(eT[:, g % 2, r * 256:(r + 1) * 256], bank[g % 2][64 * r:64 * r + 64, 0:256])
                ins.then_inc(S["eT_ok"], 1)
            for b in range(-2, B + 1):
                for k in range(16):
                    step = 16 * b + k + 1
                    for u in (2 * step, 2 * step + 1):
                        if 0 <= u < 32 * B:
                            act.wait_ge(S["st_ps"], u + 1)
                            if step >= NPROB:
                                act.wait_ge(S["pv_done"], step - NPROB + 1)
                            nc.scalar.activation(prob[:, step % NPROB, u % 2, :], bank[u % NST][:], ACT.Exp,
                                                 scale=SC).then_inc(S["exp_done"], 1)
                    if k % 4 == 3 and 0 <= b < B:
                        pair = k // 4
                        act.wait_ge(S["pv_done"], 16 * b + k + 1)
                        if b >= 2:
                            act.wait_ge(S["vo_ps"], J * (b - 1))
                            act.wait_ge(S["srow_in"], 32 * (b - 1))
                        nc.scalar.copy(ctxT[:, b % 2, pair, :], bank[5][:]).then_inc(S["ctx_copied"], 1)
                    for a in aux_at(b, k):
                        kind, ab, i = a
                        if kind == "xT":
                            act.wait_ge(S["xT_ps"], ab + 1)
                            if ab >= 1:
                                act.wait_ge(S["proj_ps"], 4 * ab)
                            nc.scalar.copy(xs[:, 0, :], ring(a)[:]).then_inc(S["x_hi"], 1)
                        if kind == "xT2":
                            act.wait_ge(S["xT2_ps"], ab + 1)
                            if ab >= 1:
                                act.wait_ge(S["up_ps"], NE * ab)
                            nc.scalar.copy(xs[:, 1, :], ring(a)[:]).then_inc(S["x2_hi"], 1)
                        if kind == "down":
                            act.wait_ge(S["dn_ps"], NE // 2 * ab + i + 1)
                            nc.scalar.activation(hid[:, 2 * i, :], ring(a)[:], ACT.Identity, bias=b2_f[:, i:i + 1]).then_inc(S["dn_ok"], 1)
                        if kind == "up":
                            u = NE * ab + i
                            act.wait_ge(S["up_ps"], u + 1)
                            if ab >= 1:
                                act.wait_ge(S["bk_ps"], J * ab)
                            nc.scalar.activation(hid[:, i, :], ring(a)[:], ACT.Relu, bias=b1_f[:, i:i + 1]).then_inc(S["relu_done"], 1)
                        if kind == "proj":
                            act.wait_ge(S["proj_ps"], 4 * ab + i + 1)
                            if ab >= 1:
                                for g in range(4):
                                    act.wait_ge(S[f"stack_{g}"], 96 * ab)
                            nc.scalar.copy(qk_h[:, i, :], ring(a)[:]).then_inc(S["qk_hi"], 1)
                        if kind == "mt":
                            act.wait_ge(S["mt_ps"], 2 * ab + i + 1)
                            if ab >= 1:
                                act.wait_ge(S["m_in"], 32 * ab - 16 + 16 * i)
                            nc.scalar.mul(negm[:, i, :], ring(a)[0:4 * J, 0:128], -1.0).then_inc(S["negm_ready"], 1)
                    if (b, k) in gate_exps:
                        act.wait_ge(S["gd_ready"], gate_exps.index((b, k)) + 1)
                        nc.scalar.activation(gs[:, 5, :], gs[:, 4, :], ACT.Exp).then_inc(S["ge_ready"], 1)

        @block.vector
        def _(dve):
            V = nc.vector
            chain = [0]

            def link(ins):
                chain[0] += 1
                ins.then_inc(S["dve_chain"], 1)
                dve.wait_ge(S["dve_chain"], chain[0])

            def wrap_clamp(f, tmp, size):
                link(V.tensor_scalar(tmp, f, 0.0, float(size), ALU.is_lt, ALU.mult))
                link(V.tensor_tensor(f, f, tmp, ALU.add))
                link(V.tensor_scalar(f, f, 0.0, float(size - 1), ALU.max, ALU.min))

            dve.wait_ge(S["ids_in"], 16)
            f, t = idf[:, 0, :], idf[:, 1, :]
            link(V.tensor_copy(f, ids[:, 0, :]))
            wrap_clamp(f, t, VOCAB)
            V.tensor_copy(ids[:, 1, :], f).then_inc(S["ids_ok"], 1)
            dve.wait_ge(S["ids_ok"], 1)
            link(V.tensor_scalar(ids[:, 2, :], ids[:, 1, :], 6, None, ALU.logical_shift_right))
            V.tensor_copy(hi_bf[:], ids[:, 2, :]).then_inc(S["hi_ok"], 1)
            link(V.tensor_scalar(ids[:, 3, :], ids[:, 1, :], LO - 1, None, ALU.bitwise_and))
            link(V.tensor_copy(idf[:, 2, :], ids[:, 3, :]))
            dve.wait_ge(S["cst_in"], 16)
            link(V.tensor_tensor(oh_lo[:], ramp_f[:, 0:LO].unsqueeze(1).to_broadcast([128, NC, LO]),
                                 idf[:, 2, :].unsqueeze(2).to_broadcast([128, NC, LO]), ALU.is_equal))
            V.memset(zrow[:], 0.0).then_inc(S["zero_set"], 1)
            V.memset(ones_f[:], 1.0).then_inc(S["b_set"], 1)
            V.memset(vo_blk[:], 0.0).then_inc(S["b_set"], 1)
            dve.wait_ge(S["tab_in"], 16)
            link(V.tensor_copy(tab_f[:, 0, :], tab_i[:]))
            wrap_clamp(tab_f[:, 0, :], tab_f[:, 1, :], NR)
            V.tensor_copy(tab[:], tab_f[:, 0, :]).then_inc(S["tab_ok"], 1)
            V.tensor_copy(minus_lower[:], minus_lower_f).then_inc(S["cons_ok"], 1)
            V.memset(ones_bf[:], 1.0).then_inc(S["cons_ok"], 1)
            V.memset(ctile_bf[:], float(TS)).then_inc(S["cons_ok"], 1)
            link(V.memset(zero_nr[:], 0.0))
            dve.wait_ge(S["hi_in"], 16)
            V.tensor_scalar(ohT[:], hi_b[:], part_f[0:HI, 0:1], None, ALU.is_equal).then_inc(S["ohT_ok"], 1)
            per = 512 // LO
            for q in range(NC // per):
                dve.wait_ge(S["looked"], q + 1)
                v = oh_lo[:, q * per:(q + 1) * per, :].rearrange("p c l -> p (c l)")
                last = V.tensor_tensor(v, bank[q][:], v, ALU.mult)
            link(last)
            link(V.tensor_reduce(rule[:], oh_lo[:], AX.X, ALU.add))
            link(V.tensor_tensor(oh[:], ramp_f[:, 0:NR].unsqueeze(2).to_broadcast([128, NR, NC]),
                                 rule[:].unsqueeze(1).to_broadcast([128, NR, NC]), ALU.is_equal))
            dve.wait_ge(S["again_ok"], 1)
            V.tensor_tensor_scan(run[:].rearrange("p r c -> p (r c)"), again.rearrange("p r c -> p (r c)"),
                                 oh[:].rearrange("p r c -> p (r c)"), 0.0, ALU.mult, ALU.add).then_inc(S["run_ok"], 1)
            dve.wait_ge(S["ranked"], 1)
            link(V.tensor_scalar(cnt_i[:, 0, :], bank[7][:, 0:NR], float(TS - 1), None, ALU.add))
            link(V.tensor_scalar(cnt_i[:, 1, :], cnt_i[:, 0, :], 7, None, ALU.logical_shift_right))
            link(V.tensor_copy(cnt[:, 0, :], cnt_i[:, 1, :]))
            link(V.tensor_tensor_scan(cnt[:, 1, :], cnt[:, 0, :], zero_nr[:], 0.0, ALU.add, ALU.add))
            V.tensor_tensor(tbase[:], cnt[0:1, 1, :], cnt[0:1, 0, :], ALU.subtract).then_inc(S["tb_ok"], 1)
            for i in range(2):
                link(V.tensor_scalar(cnt[:, 2 + i, :], cnt[:, 1, :], part_f[:, i:i + 1], None, ALU.is_le))
            link(V.tensor_reduce(trule[:], cnt[:, 2:4, :], AX.X, ALU.add))
            V.tensor_scalar(trule[:], trule[:], float(NR - 1), float(D), ALU.min, ALU.mult).then_inc(S["trule_ok"], 1)
            dve.wait_ge(S["placed"], 1)
            for q in range(NCH):
                w = min(CB, NC - q * CB)
                o = oh[:].rearrange("p r c -> p c r")[:, q * CB:q * CB + w, :]
                last = V.tensor_tensor(sel[:, q * CB:q * CB + w, :], bank[q][:, 0:w * NR].rearrange("p (c r) -> p c r", r=NR), o, ALU.mult)
            link(last)
            link(V.tensor_reduce(idf[:, 0, :], sel, AX.X, ALU.add))
            link(V.tensor_copy(pos_t[:, 0, :], idf[:, 0, :]))
            link(V.tensor_scalar(pos_t[:, 1, :], pos_t[:, 0, :], 9, 9, ALU.logical_shift_right, ALU.logical_shift_left))
            link(V.tensor_scalar(pos_t[:, 2, :], pos_t[:, 0, :], 127, 2, ALU.bitwise_and, ALU.logical_shift_left))
            link(V.tensor_scalar(pos_t[:, 3, :], pos_t[:, 0, :], 7, 3, ALU.logical_shift_right, ALU.bitwise_and))
            link(V.tensor_tensor(pos_t[:, 4, :], pos_t[:, 1, :], pos_t[:, 2, :], ALU.bitwise_or))
            V.tensor_tensor(pos[:], pos_t[:, 4, :], pos_t[:, 3, :], ALU.bitwise_or).then_inc(S["pos_ok"], 1)
            dve.wait_ge(S["trowed"], 1)
            V.tensor_copy(trow[:], bank[7][0:1, 0:256]).then_inc(S["trow_ok"], 1)
            dve.wait_ge(S["wq_h"], 1)
            V.tensor_tensor(wqk_l[:].rearrange("p o n -> p (o n)"), bank[7][:],
                            wqk_h[:].rearrange("p o n -> p (o n)").bitcast(F32), ALU.subtract).then_inc(S["wq_ok"], 1)
            dve.wait_ge(S["w1_h"], 3)
            V.tensor_tensor(w1_l[:], w1_f, w1_h[:].bitcast(F32), ALU.subtract).then_inc(S["w_ok"], 1)
            V.tensor_tensor(wg_l[:], wg_f[:], wg_h[:].bitcast(F32), ALU.subtract).then_inc(S["w_ok"], 1)
            for hh in range(2):
                r = slice(64 * hh, 64 * hh + 64)
                V.tensor_tensor(vo_blk[r, :, hh, :], vo_blk[r, :, hh, :], vo_row0[r, :, :], ALU.subtract).then_inc(S["w_ok"], 1)
            V.tensor_scalar(gi[:], ramp_f[:, 0:NE], 1000.0, None, ALU.add).then_inc(S["w_ok"], 1)
            for g in range(NG):
                dve.wait_ge(S["y_ps"], g + 1)
                if g >= 4:
                    dve.wait_ge(y_out_sem[g % 4], 16 * (g // 4))
                V.tensor_copy(y_out[:, g % 4, :], bank[2 + g % 2][:, 0:GT * D]).then_inc(S["y_ok"], 1)
            dve.wait_ge(S["scattered"], 16 * NC)

            def layernorm(b, done):
                if done == "xn_ready":
                    dve.wait_ge(y_loaded[b], 16 * J)
                else:
                    dve.wait_ge(S["h1_ready"], J * (b + 1))
                h4 = hbuf[:, b * J:(b + 1) * J, :]
                wide = [128, J, D]
                s_ = [ln_s[:, i, :] for i in range(8)]
                link(V.tensor_reduce(s_[0], h4, AX.X, ALU.add))
                link(V.tensor_scalar(s_[1], s_[0], 1.0 / D, None, ALU.mult))
                yield
                link(V.tensor_tensor(ln_c[:], h4, s_[1].unsqueeze(2).to_broadcast(wide), ALU.subtract))
                yield
                link(V.tensor_tensor(ln_q[:], ln_c[:], ln_c[:], ALU.mult))
                yield
                link(V.tensor_reduce(s_[2], ln_q[:], AX.X, ALU.add))
                link(V.tensor_scalar(s_[3], s_[2], 1.0 / D, EPS, ALU.mult, ALU.add))
                link(V.tensor_scalar(s_[4].bitcast(I32), s_[3].bitcast(I32), 1, None, ALU.logical_shift_right))
                yield
                link(V.tensor_scalar(s_[5].bitcast(I32), s_[4].bitcast(I32), -1.0, float(0x5F3759DF), ALU.mult, ALU.add))
                for i in range(3):
                    if i == 1:
                        yield
                    link(V.scalar_tensor_tensor(s_[6], s_[5], -0.5, s_[5], ALU.mult, ALU.mult))
                    link(V.tensor_tensor(s_[7], s_[6], s_[3], ALU.mult))
                    link(V.scalar_tensor_tensor(s_[5], s_[7], 1.5, s_[5], ALU.add, ALU.mult))
                yield
                V.tensor_tensor(xn[:, b * J:(b + 1) * J, :, :], ln_c[:].unsqueeze(2).to_broadcast([128, J, 2, D]),
                                s_[5].unsqueeze(2).unsqueeze(3).to_broadcast([128, J, 2, D]), ALU.mult).then_inc(S[done], 1)

            def gate(b, logits):
                dve.wait_ge(S["gate_ps"], b + 1)
                l, eq, cand, oh1, l2, oh2, t1, t2 = (gt[:, i, :, :] for i in range(8))
                m1, i1, m2, i2, dd, ee, w1_, w2_ = (gs[:, i, :] for i in range(8))
                w3 = [128, J, NE]
                ramp3 = ramp_f[:, 0:NE].unsqueeze(1).to_broadcast(w3)
                gi3 = gi[:].unsqueeze(1).to_broadcast(w3)

                def over_e(v):
                    return v.unsqueeze(2).to_broadcast(w3)

                V.tensor_tensor(l, logits[:, 0:J * NE].rearrange("p (j e) -> p j e", e=NE),
                                bg_f[:, 0, :].unsqueeze(1).to_broadcast(w3), ALU.add).then_inc(S["gate_used"], 1)
                dve.wait_ge(S["gate_used"], b + 1)
                yield
                link(V.tensor_tensor(l, l, bg_f[:, 1, :].unsqueeze(1).to_broadcast(w3), ALU.add))

                def pick(l_, m_, i_, oh_):
                    link(V.tensor_reduce(m_, l_, AX.X, ALU.max))
                    link(V.tensor_tensor(eq, l_, over_e(m_), ALU.is_equal))
                    yield
                    link(V.scalar_tensor_tensor(cand, eq, -1000.0, gi3, ALU.mult, ALU.add))
                    link(V.tensor_reduce(i_, cand, AX.X, ALU.min))
                    link(V.tensor_tensor(oh_, ramp3, over_e(i_), ALU.is_equal))

                yield from pick(l, m1, i1, oh1)
                yield
                link(V.scalar_tensor_tensor(l2, oh1, -3.0e38, l, ALU.mult, ALU.add))
                yield from pick(l2, m2, i2, oh2)
                V.tensor_tensor(dd, m2, m1, ALU.subtract).then_inc(S["gd_ready"], 1)
                yield
                dve.wait_ge(S["ge_ready"], b + 1)
                link(V.tensor_scalar(w2_, ee, 1.0, None, ALU.add))
                link(V.reciprocal(w1_, w2_))
                link(V.tensor_tensor(w2_, ee, w1_, ALU.mult))
                link(V.tensor_tensor(t1, oh1, over_e(w1_), ALU.mult))
                link(V.tensor_tensor(t2, oh2, over_e(w2_), ALU.mult))
                link(V.tensor_tensor(comb[:], t1, t2, ALU.add))

            gating = iter(())
            for b in range(-2, B + 1):
                if b == -2:
                    for _ in layernorm(0, "xn_ready"):
                        pass
                parts = iter(())
                for k in range(16):
                    if k == 0 and 0 <= b - 2 < B - 2:
                        parts = layernorm(b - 2, "xn2_ready")
                    if k == 8 and b + 3 < B:
                        parts = layernorm(b + 3, "xn_ready")
                    if (b, k) in ((B - 1, 15), (B, 9)):
                        for _ in layernorm(B - 2 if b < B else B - 1, "xn2_ready"):
                            pass
                    next(parts, None)
                    if k == 0 or k in ((9, 10, 11, 12) if b < B else (2, 3, 4, 5, 7, 11, 12, 13, 14, 15)):
                        next(gating, None)
                    for u in s_units(b, k):
                        nb = b + 1
                        n = 32 * nb + u
                        dve.wait_ge(S["s_ps"], n + 1)
                        if nb >= 1 and u % 16 == 0:
                            dve.wait_ge(S["mt_ps"], 2 * nb - 1 + u // 16)
                        V.tensor_reduce(mx[:, u // 16, u % 16:u % 16 + 1], bank[3 + n % 2][:], AX.X, ALU.max).then_inc(S["mx_done"], 1)
                    for a in aux_at(b, k):
                        kind, ab, i = a
                        if kind == "xT":
                            dve.wait_ge(S["x_hi"], ab + 1)
                            lo_rows = xs[64:128, 0, :]
                            V.tensor_tensor(lo_rows, ring(a)[64:128, :], lo_rows.bitcast(F32), ALU.subtract).then_inc(S["xs_ready"], 1)
                        if kind == "xT2":
                            dve.wait_ge(S["x2_hi"], ab + 1)
                            lo_rows = xs[64:128, 1, :]
                            V.tensor_tensor(lo_rows, ring(a)[64:128, :], lo_rows.bitcast(F32), ALU.subtract).then_inc(S["xs2_ready"], 1)
                        if kind == "gate":
                            gating = gate(ab, ring(a))
                            next(gating)
                        if kind == "back":
                            dve.wait_ge(S["bk_ps"], J * ab + i + 1)
                            folded(dve, a)
                            V.tensor_tensor(vtmp[:, term[a] % 2, :].rearrange("p (e d) -> p e d", d=D),
                                            ring(a)[:].rearrange("p (e d) -> p e d", d=D),
                                            comb[:, i, :].unsqueeze(2).to_broadcast([128, NE, D]), ALU.mult).then_inc(S["bk_used"], 1)
                        if kind == "proj":
                            dve.wait_ge(S["qk_hi"], 4 * ab + i + 1)
                            V.tensor_tensor(qk_l[:, i, :], ring(a)[:], qk_h[:, i, :].bitcast(F32), ALU.subtract).then_inc(S["qk_lo"], 1)
                        if kind == "rt":
                            dve.wait_ge(S["rt_ps"], ab + 1)
                            if ab >= 1:
                                dve.wait_ge(S["vo_used"], J * ab)
                            V.reciprocal(rsum[:].rearrange("p j t q -> p (j t q)"), ring(a)[:, 0:8 * J]).then_inc(S["rsum_ready"], 1)
                        if kind == "vo":
                            n = J * ab + i
                            dve.wait_ge(S["vo_ps"], n + 1)
                            dve.wait_ge(S["rsum_ready"], ab + 1)
                            folded(dve, a)
                            V.tensor_tensor(vtmp[:, term[a] % 2, :].rearrange("p (q t e) -> p t q e", t=2, e=D),
                                            ring(a)[:].rearrange("p (q t e) -> p t q e", t=2, e=D),
                                            rsum[:, i, :, :].unsqueeze(3).to_broadcast([128, 2, NPAIR, D]),
                                            ALU.mult).then_inc(S["vo_used"], 1)

        @block.tensor
        def _(pe):
            M = nc.tensor.matmul
            pe.wait_ge(S["ohT_ok"], 1)
            pe.wait_ge(S["tab_ok"], 1)
            cols = ohT[:].rearrange("h (p c) -> h c p", c=NC)
            per = 512 // LO
            for c in range(NC):
                last = M(bank[c // per][:, c % per * LO:(c % per + 1) * LO], cols[:, c, :], tab[:], start=True, stop=True)
                if c % per == per - 1:
                    last.then_inc(S["looked"], 1)
            pe.wait_ge(S["run_ok"], 1)
            pe.wait_ge(S["cons_ok"], 3)
            for q in range(NCH):
                w = min(CB, NC - q * CB)
                M(bank[q][:, 0:w * NR], minus_lower[:], oh[:].rearrange("p r c -> p c r")[:, q * CB:q * CB + w, :], start=True, stop=False)
                M(bank[q][:, 0:w * NR], ones_bf[:], run[:].rearrange("p r c -> p c r")[:, q * CB:q * CB + w, :], start=False, stop=False)
            M(bank[7][:, 0:NR], ones_bf[:], run[:, :, NC - 1], start=True, stop=True).then_inc(S["ranked"], 1)
            pe.wait_ge(S["tb_ok"], 1)
            for q in range(NCH):
                w = min(CB, NC - q * CB)
                last = M(bank[q][:, 0:w * NR], ctile_bf[:], tbase[:].unsqueeze(1).to_broadcast([1, w, NR]), start=False, stop=True)
            last.then_inc(S["placed"], 1)
            pe.wait_ge(S["trule_ok"], 1)
            for i in range(2):
                last = M(bank[7][0:1, i * 128:(i + 1) * 128], trule[:, i:i + 1], ident, start=True, stop=True)
            last.then_inc(S["trowed"], 1)
            pe.wait_ge(S["trow_ok"], 1)
            pe.wait_ge(S["qk_in"], 16 * 8)
            pe.wait_ge(S["cst_in"], 16)
            for o in range(4):
                last = nc.tensor.transpose(bank[7][:, o * 128:(o + 1) * 128], qk_nat[:, o, :, :].rearrange("p t d -> p (t d)"), ident)
            last.then_inc(S["wq_ps"], 1)
            pe.wait_ge(S["rules_in"], 16)
            pe.wait_ge(S["scatters_issued"], 1)
            for _ in range(WARM):
                M(bank[5][:, 0:384], ident, cst[:, 0:384], start=True, stop=True)
            for g in range(NG + 1):
                if g < NG:
                    at_next = nc.values_load_multi_w_load_instructions(
                        trow[0:1, g * GT:(g + 1) * GT], engines=[mybir.EngineType.PE], min_val=0, max_val=(NR - 1) * D,
                        skip_runtime_bounds_check_because="clamped above")[1]
                    pe.wait_ge(e_in_sem[g % NE_IN], 16 * (g // NE_IN + 1))
                    if g >= 2:
                        pe.wait_ge(S["eT_ok"], g - 1)
                    for i in range(GT // 2):
                        last = nc.tensor.transpose(bank[g % 2][:, i * 128:(i + 1) * 128],
                                                   e_in[:, g % NE_IN, 2 * i * D:2 * (i + 1) * D], ident)
                    last.then_inc(S["eT_ps"], 1)
                if g >= 1:
                    q = g - 1
                    pe.wait_ge(S["eT_ok"], q + 1)
                    if q >= 2:
                        pe.wait_ge(S["y_ok"], q - 1)
                    for s in range(GT):
                        col = s % 2 * 256 + s // 2 * 128
                        last = M(bank[2 + q % 2][:, s * D:(s + 1) * D], eT[:, q % 2, col:col + TS],
                                 r_sb[:, bass.ds(at[s], D)], start=True, stop=True)
                    last.then_inc(S["y_ps"], 1)
                at = at_next

            pe.wait_ge(S["wq_ok"], 1)
            pe.wait_ge(S["w_ok"], 5)

            def aux(a):
                kind, b, i = a
                out_ = ring(a)
                if kind == "xT":
                    pe.wait_ge(S["xn_ready"], b + 1)
                if kind == "xT2":
                    pe.wait_ge(S["xn2_ready"], b + 1)
                drained(pe, a)
                if kind in ("xT", "xT2"):
                    for j in range(J):
                        last = nc.tensor.transpose(out_[:, j * 128:(j + 1) * 128],
                                                   xn[:, b * J + j, :, :].rearrange("p t d -> p (t d)"), ident)
                    last.then_inc(S[kind + "_ps"], 1)
                if kind == "proj":
                    pe.wait_ge(S["xs_ready"], b + 1)
                    M(out_[:], wqk_h[:, i, :], xs[:, 0, :], start=True, stop=False)
                    M(out_[:], wqk_l[:, i, :], xs[:, 0, :], start=False, stop=True).then_inc(S["proj_ps"], 1)
                if kind == "gate":
                    pe.wait_ge(S["xs2_ready"], b + 1)
                    for j in range(J):
                        o = out_[:, j * NE:(j + 1) * NE]
                        M(o, xs[:, 1, j * 128:(j + 1) * 128], wg_h[:], start=True, stop=False)
                        last = M(o, xs[:, 1, j * 128:(j + 1) * 128], wg_l[:], start=False, stop=True)
                    last.then_inc(S["gate_ps"], 1)
                if kind == "up":
                    M(out_[:], w1_h[:, i * HID:(i + 1) * HID], xs[:, 1, :], start=True, stop=False)
                    M(out_[:], w1_l[:, i * HID:(i + 1) * HID], xs[:, 1, :], start=False, stop=True).then_inc(S["up_ps"], 1)
                if kind == "down":
                    pe.wait_ge(S["relu_done"], NE * b + 2 * i + 2)
                    for t in range(2):
                        last = M(out_[64 * t:64 * t + 64, :], w2_f[:, 2 * i + t, :], hid[:, 2 * i + t, :], start=True, stop=True)
                    last.then_inc(S["dn_ps"], 1)
                if kind == "back":
                    pe.wait_ge(S["dn_ok"], NE // 2 * (b + 1))
                    for p in range(NE // 2):
                        last = nc.tensor.transpose(out_[:, p * 128:(p + 1) * 128], hid[:, 2 * p, i * 128:(i + 1) * 128], ident)
                    last.then_inc(S["bk_ps"], 1)
                if kind == "mt":
                    pe.wait_ge(S["mx_done"], 32 * b + 16 * (i + 1))
                    nc.tensor.transpose(out_[0:4 * J, 0:128], mx[:, i, :], ident).then_inc(S["mt_ps"], 1)
                if kind == "rt":
                    pe.wait_ge(S["srow_in"], 32 * (b + 1))
                    for j in range(J):
                        last = nc.tensor.transpose(out_[:, j * 8:(j + 1) * 8], srow[:, j * 128:(j + 1) * 128], ident[0:8, 0:8])
                    last.then_inc(S["rt_ps"], 1)
                if kind == "vo":
                    pe.wait_ge(S["ctx_copied"], NPAIR * (b + 1))
                    for pair in range(NPAIR):
                        last = M(out_[:, pair * 128:(pair + 1) * 128], ctxT[:, b % 2, pair, i * 128:(i + 1) * 128],
                                 vo_blk[:, pair, :, :].rearrange("p t e -> p (t e)"), start=True, stop=True)
                    last.then_inc(S["vo_ps"], 1)

            for b in range(-2, B + 1):
                for k in range(16):
                    step = 16 * b + k + 1
                    for u in (2 * step, 2 * step + 1):
                        if 0 <= u < 32 * B:
                            ub, pair, ut, hh = u // 32, u // 8 % 4, u // 2 % 4, u % 2
                            h = 2 * pair + hh
                            pe.wait_ge(S["m_in"], 32 * ub + 16 * (h // 4 + 1))
                            if u >= NST:
                                pe.wait_ge(S["exp_done"], u - NST + 1)
                            M(bank[u % NST][:], ks[:, ub % 2, h, ut * 128:(ut + 1) * 128], qs[:, ub % 2, h, :],
                              start=True, stop=True).then_inc(S["st_ps"], 1)
                    todo = list(s_units(b, k))

                    def score_tile():
                        if not todo:
                            return
                        u = todo.pop(0)
                        nb = b + 1
                        n = 32 * nb + u
                        h, tt = u // J, u % J
                        pe.wait_ge(S[f"stack_{h // 2}"], 96 * (nb + 1))
                        if n >= 2:
                            pe.wait_ge(S["mx_done"], n - 1)
                        M(bank[3 + n % 2][:], qs[0:96, nb % 2, h, tt * 128:(tt + 1) * 128], ks[0:96, nb % 2, h, :],
                          start=True, stop=True).then_inc(S["s_ps"], 1)

                    score_tile()
                    if 0 <= b < B:
                        pair, ut = k // 4, k % 4
                        pe.wait_ge(S["exp_done"], 32 * b + 2 * k + 2)
                        pe.wait_ge(S["xa_ready"], b + 1)
                        if ut == 0 and NPAIR * b + pair >= 1:
                            pe.wait_ge(S["ctx_copied"], NPAIR * b + pair)
                        for hh in range(2):
                            last = M(bank[5][64 * hh:64 * hh + 64, :], xa[:, b * J + ut, :],
                                     prob[:, (16 * b + k) % NPROB, hh, :], start=(ut == 0), stop=(ut == J - 1))
                        last.then_inc(S["pv_done"], 1)
                    score_tile()
                    for a in aux_at(b, k):
                        aux(a)
                    score_tile()


INPUTS = ['x', 'L0_tok_base_embeddings', 'L0_tok_rule_transform', 'L0_tok_token_rules', 'L0_attn_Q', 'L0_attn_K',
          'L0_attn_VO', 'L0_ffn_Wg', 'L0_ffn_bg', 'L0_ffn_bias', 'L0_ffn_W1', 'L0_ffn_b1', 'L0_ffn_W2', 'L0_ffn_b2']


def kernel(**inputs):
    import concourse.bacc as bacc
    from concourse.bass_utils import run_bass_kernel_spmd

    nc = bacc.Bacc("TRN2", target_bir_lowering=False, num_devices=1)
    arrays = {f"in_{name}": np.ascontiguousarray(inputs[name]) for name in INPUTS}
    arrays["in_consts"] = shape_constants()
    args = [nc.dram_tensor(name, a.shape, mybir.dt.from_np(a.dtype), kind="ExternalInput").ap() for name, a in arrays.items()]
    batch, seq = inputs["x"].shape
    width = inputs["L0_tok_base_embeddings"].shape[1]
    out = nc.dram_tensor("out", (batch, seq, width), mybir.dt.float32, kind="ExternalOutput").ap()
    lm_tower_kernel(nc, *args, out)
    return run_bass_kernel_spmd(nc, [arrays], core_ids=[0]).results[0]["out"]
```
